# Optimizing a Trainium2 kernel written in Bass

```python
import numpy as np
import jax
import jax.numpy as jnp

def _softmax(x, axis=-1):
    return jax.nn.softmax(x, axis=axis)

def _gelu(x):
    return jax.nn.gelu(x, approximate=True)

def _silu(x):
    return jax.nn.silu(x)

def _sigmoid(x):
    return jax.nn.sigmoid(x)

def _layernorm(x, axis=-1, eps=1e-05):
    m = jnp.mean(x, axis=axis, keepdims=True)
    v = jnp.var(x, axis=axis, keepdims=True)
    return (x - m) / jnp.sqrt(v + eps)

def _scatter_add(tgt, idx, src, axis=0):
    return tgt.at[idx].add(src)

def _segment_sum(src, seg, n):
    return jax.ops.segment_sum(src, seg, n)
kernel_name = 'mk_gnn_preln_d2_gnn_r8_4b206e'

def setup_inputs(seed: int=0):
    np.random.seed(seed)
    _w = jnp.asarray

    def _rec_inputs():
        import jax
        import jax.numpy as jnp
        _gk = jax.random.key(seed)
        x = -0.0001006 + 1 * jax.random.normal(jax.random.fold_in(_gk, 1), (12500, 96), jnp.float32)
        src = jax.random.randint(jax.random.fold_in(_gk, 2), (200000,), 0, 12500, jnp.int32)
        dst = jnp.minimum((12500 * jax.random.uniform(jax.random.fold_in(_gk, 3), (200000,)) ** 2.0).astype(jnp.int32), 99999)
        _o = jnp.argsort(dst, stable=True)
        src = src[_o]
        dst = dst[_o]
        edge_attr_32 = 0.000196303 + 1.00016 * jax.random.normal(jax.random.fold_in(_gk, 11), (200000, 32), jnp.float32)
        edge_weight = jax.random.uniform(jax.random.fold_in(_gk, 13), (200000,), jnp.float32, 0.0, 0.999998)
        return (x, src, dst, edge_attr_32, edge_weight)
    x, src, dst, edge_attr_32, edge_weight = _rec_inputs()

    def _L0_gnn_setup():
        import jax, jax.numpy as jnp
        import numpy as np
        N_NODES = 6250
        N_EDGES = 100000
        FEAT = 96

        def gcn_conv(x, edge_index, edge_weight, W, b, n_nodes):
            row, col = (edge_index[0], edge_index[1])
            loop = jnp.arange(n_nodes, dtype=edge_index.dtype)
            row = jnp.concatenate([row, loop])
            col = jnp.concatenate([col, loop])
            ew = jnp.concatenate([edge_weight, jnp.ones((n_nodes,), x.dtype)])
            deg = jax.ops.segment_sum(ew, col, num_segments=n_nodes)
            dinv = jnp.where(deg > 0, jax.lax.rsqrt(deg), jnp.zeros_like(deg))
            norm = dinv[row] * ew * dinv[col]
            h = x @ W
            msg = h[row] * norm[:, None]
            out = jax.ops.segment_sum(msg, col, num_segments=n_nodes)
            return out + b
        key = jax.random.key(seed)
        k = jax.random.split(key, 6)
        x = jax.random.normal(k[0], (N_NODES, FEAT), dtype=jnp.float32)
        edge_index = jax.random.randint(k[1], (2, N_EDGES), 0, N_NODES, dtype=jnp.int64)
        edge_weight = jax.random.uniform(k[2], (N_EDGES,), dtype=jnp.float32)
        s = 1.0 / np.sqrt(FEAT)
        W1 = jax.random.normal(k[3], (FEAT, FEAT), dtype=jnp.float32) * s
        W2 = jax.random.normal(k[4], (FEAT, FEAT), dtype=jnp.float32) * s
        b1 = jnp.zeros((FEAT,), dtype=jnp.float32)
        b2 = jnp.zeros((FEAT,), dtype=jnp.float32)
        return {'x': x, 'edge_index': edge_index, 'edge_weight': edge_weight, 'W1': W1, 'b1': b1, 'W2': W2, 'b2': b2}
    _L0_gnn_all = _L0_gnn_setup()
    _L0_gnn_in = {k: v for k, v in _L0_gnn_all.items() if k in ('W1', 'b1', 'W2', 'b2')}
    del _L0_gnn_all

    def _L1_gnn_setup():
        import jax, jax.numpy as jnp
        import numpy as np
        N_NODES = 6250
        N_EDGES = 100000
        IN_DIM = 96
        OUT_DIM = 96
        EDGE_DIM = 32
        BN_EPS = 1e-05
        key = jax.random.key(seed)
        ks = jax.random.split(key, 12)
        x = jax.random.normal(ks[0], (N_NODES, IN_DIM), dtype=jnp.float32)
        edge_index = jax.random.randint(ks[1], (2, N_EDGES), 0, N_NODES, dtype=jnp.int64)
        edge_attr = jax.random.normal(ks[2], (N_EDGES, EDGE_DIM), dtype=jnp.float32)
        We = jax.random.normal(ks[3], (EDGE_DIM, IN_DIM), dtype=jnp.float32) / np.sqrt(EDGE_DIM)
        be = jnp.zeros((IN_DIM,), dtype=jnp.float32)
        W1 = jax.random.normal(ks[4], (IN_DIM, OUT_DIM), dtype=jnp.float32) / np.sqrt(IN_DIM)
        b1 = jnp.zeros((OUT_DIM,), dtype=jnp.float32)
        W2 = jax.random.normal(ks[5], (OUT_DIM, OUT_DIM), dtype=jnp.float32) / np.sqrt(OUT_DIM)
        b2 = jnp.zeros((OUT_DIM,), dtype=jnp.float32)
        gamma = jnp.ones((OUT_DIM,), dtype=jnp.float32)
        beta = jnp.zeros((OUT_DIM,), dtype=jnp.float32)
        return {'x': x, 'edge_index': edge_index, 'edge_attr': edge_attr, 'We': We, 'be': be, 'W1': W1, 'b1': b1, 'W2': W2, 'b2': b2, 'gamma': gamma, 'beta': beta}
    _L1_gnn_all = _L1_gnn_setup()
    _L1_gnn_in = {k: v for k, v in _L1_gnn_all.items() if k in ('We', 'be', 'W1', 'b1', 'W2', 'b2', 'gamma', 'beta')}
    del _L1_gnn_all
    return {'x': x, 'src': src, 'dst': dst, 'edge_attr_32': edge_attr_32, 'edge_weight': edge_weight, 'L0_gnn_W1': _L0_gnn_in['W1'], 'L0_gnn_b1': _L0_gnn_in['b1'], 'L0_gnn_W2': _L0_gnn_in['W2'], 'L0_gnn_b2': _L0_gnn_in['b2'], 'L1_gnn_We': _L1_gnn_in['We'], 'L1_gnn_be': _L1_gnn_in['be'], 'L1_gnn_W1': _L1_gnn_in['W1'], 'L1_gnn_b1': _L1_gnn_in['b1'], 'L1_gnn_W2': _L1_gnn_in['W2'], 'L1_gnn_b2': _L1_gnn_in['b2'], 'L1_gnn_gamma': _L1_gnn_in['gamma'], 'L1_gnn_beta': _L1_gnn_in['beta']}

def reference(x, src, dst, edge_attr_32, edge_weight, L0_gnn_W1, L0_gnn_b1, L0_gnn_W2, L0_gnn_b2, L1_gnn_We, L1_gnn_be, L1_gnn_W1, L1_gnn_b1, L1_gnn_W2, L1_gnn_b2, L1_gnn_gamma, L1_gnn_beta):
    import jax
    import jax.numpy as jnp

    def _L0_gnn_ref(x, edge_index, edge_weight, W1, b1, W2, b2):
        import jax, jax.numpy as jnp
        import numpy as np
        N_NODES = 6250
        N_EDGES = 100000
        FEAT = 96

        def gcn_conv(x, edge_index, edge_weight, W, b, n_nodes):
            row, col = (edge_index[0], edge_index[1])
            loop = jnp.arange(n_nodes, dtype=edge_index.dtype)
            row = jnp.concatenate([row, loop])
            col = jnp.concatenate([col, loop])
            ew = jnp.concatenate([edge_weight, jnp.ones((n_nodes,), x.dtype)])
            deg = jax.ops.segment_sum(ew, col, num_segments=n_nodes)
            dinv = jnp.where(deg > 0, jax.lax.rsqrt(deg), jnp.zeros_like(deg))
            norm = dinv[row] * ew * dinv[col]
            h = x @ W
            msg = h[row] * norm[:, None]
            out = jax.ops.segment_sum(msg, col, num_segments=n_nodes)
            return out + b
        n = x.shape[0]
        h = gcn_conv(x, edge_index, edge_weight, W1, b1, n)
        h = jax.nn.relu(h)
        h = gcn_conv(h, edge_index, edge_weight, W2, b2, n)
        return jax.nn.log_softmax(h, axis=1)

    def _L1_gnn_ref(x, edge_index, edge_attr, We, be, W1, b1, W2, b2, gamma, beta):
        import jax, jax.numpy as jnp
        import numpy as np
        N_NODES = 6250
        N_EDGES = 100000
        IN_DIM = 96
        OUT_DIM = 96
        EDGE_DIM = 32
        BN_EPS = 1e-05
        src = edge_index[0]
        dst = edge_index[1]
        msg = jax.nn.relu(x[src] + edge_attr @ We + be)
        aggr = jax.ops.segment_sum(msg, dst, num_segments=x.shape[0])
        h = x + aggr
        h = jax.nn.relu(h @ W1 + b1) @ W2 + b2
        mean = jnp.mean(h, axis=0)
        var = jnp.mean(jnp.square(h - mean), axis=0)
        h = (h - mean) * jax.lax.rsqrt(var + BN_EPS) * gamma + beta
        return jax.nn.relu(h)
    edge_index = jnp.stack([src, dst])
    h = jnp.maximum(_layernorm(x, axis=-1), 0.0)
    x = x + _L0_gnn_ref(h, edge_index, edge_weight, L0_gnn_W1, L0_gnn_b1, L0_gnn_W2, L0_gnn_b2)
    h = jnp.maximum(_layernorm(x, axis=-1), 0.0)
    x = x + _L1_gnn_ref(h, edge_index, edge_attr_32, L1_gnn_We, L1_gnn_be, L1_gnn_W1, L1_gnn_b1, L1_gnn_W2, L1_gnn_b2, L1_gnn_gamma, L1_gnn_beta)
    return x

_drawn_inputs = setup_inputs


def setup_inputs(seed=0):
    import zlib

    import numpy as np

    out = dict(_drawn_inputs(seed))
    spreads = {'L0_gnn_b1': (0.0, 0.464),
     'L0_gnn_b2': (0.0, 0.367),
     'L1_gnn_be': (0.0, 0.47),
     'L1_gnn_b1': (0.0, 0.8),
     'L1_gnn_b2': (0.0, 0.8),
     'L1_gnn_gamma': (1.0, 0.2),
     'L1_gnn_beta': (0.0, 0.506)}
    factors = {'edge_weight': 6.87}
    for name, (base, spread) in spreads.items():
        noise = np.random.default_rng([zlib.crc32(name.encode()), seed]).standard_normal(out[name].shape)
        drawn = base * np.exp(spread * noise) if base else spread * noise
        out[name] = jnp.asarray(drawn.astype(out[name].dtype))
    for name, factor in factors.items():
        out[name] = (out[name] * factor).astype(out[name].dtype)
    return out
```

```python
import concourse.bass as bass
from concourse import mybir
from contextlib import ExitStack

F32 = mybir.dt.float32
I32 = mybir.dt.int32
ALU = mybir.AluOpType
ACT = mybir.ActivationFunctionType
AX = mybir.AxisListType


def build_gnn(nc, x, src, dst, edge_attr, edge_weight, c1_w, c1_b, c2_w, c2_b,
              we, be, g1_w, g1_b, g2_w, g2_b, gamma, beta, out):
    N, F = x.shape
    E = src.shape[0]
    KE = edge_attr.shape[1]
    P = 128
    G = 4
    GE = G * P
    NS = -(-E // GE)
    FULL = E // GE
    TP = (E - FULL * GE) // G
    U = 3
    ITERS = FULL // U
    CH = -(-NS // P)
    LASTQ = NS - (CH - 1) * P
    W = 128
    AL = 32
    WA = W // AL
    NA = -(-N // AL)
    CA = -(-NA // P)
    J = 100
    PN = N // J
    PK = PN // 16 * 16
    JC = 20
    NC = J // JC
    JQ = 4
    NQ = J // JQ
    QC = JC // JQ
    SW = 500
    NW = N // SW
    FAR = -float(1 << 20)
    EPS = 1e-5
    TINY = 1.2e-38
    PASSES = 3
    assert FULL == NS - 1 and FULL % (2 * U) == 0 and TP * G == E - FULL * GE and TP % 16 == 0
    assert N % J == 0 and N % SW == 0 and J % JC == 0 and JC % JQ == 0 and NA + WA <= 512

    table = [nc.dram_tensor(f"table{p}", (N, F), F32).ap() for p in range(PASSES)]
    deg_lin = nc.dram_tensor("deg_lin", (NA * AL,), F32).ap()

    ctx = ExitStack()
    with ctx:
        def sb(name, shape, dt=F32):
            return ctx.enter_context(nc.sbuf_tensor(name, shape, dt))

        def sem(name):
            return ctx.enter_context(nc.semaphore(name))

        x_sb = sb("x_sb", [PN, J, F])
        tab_t = sb("tab", [P, J * F])
        tab = tab_t[0:PN, :].rearrange("p (j f) -> p j f", j=J)
        acc_t = sb("acc", [P, N + W])
        acc = acc_t[0:F, :]
        acc_j = acc[:, 0:N].rearrange("f (p j) -> f j p", j=J)
        edge = sb("edge", [P, NS, 4 * G])
        part = lambda t, k, n: t[:, k * n:(k + 1) * n]
        row = [part(tab_t, k, CH * GE).rearrange("q (c e) -> q c e", c=CH) for k in range(4)]
        row_src, row_rel, row_wgt, row_far = row
        dst_i = part(acc_t, 0, CH * GE).bitcast(I32).rearrange("q (c e) -> q c e", c=CH)
        src_i = part(acc_t, 1, CH * GE).bitcast(I32).rearrange("q (c e) -> q c e", c=CH)
        row_dst = part(acc_t, 2, CH * GE).rearrange("q (c e) -> q c e", c=CH)
        off = 3 * CH * GE
        col_b = acc_t[:, off:off + NS * G]
        col_a = acc_t[:, off + NS * G:off + 2 * NS * G]
        col_i = part(acc_t, 0, NS * G).bitcast(I32)
        col_i2 = part(acc_t, 1, NS * G).bitcast(I32)
        deg_sb = part(acc_t, 2, NS * G)[0:AL, 0:NA]
        least = sb("least", [P, CH])
        most = sb("most", [P, CH])
        win_i = sb("win_i", [P, CH], I32)
        base_i = sb("base_i", [P, CH], I32)
        win_f = sb("win_f", [P, CH])
        base_f = sb("base_f", [P, CH])
        span_f = sb("span_f", [P, CH])
        win_row = sb("win_row", [1, CH * P], I32)
        flag_f = sb("flag_f", [1, 1])
        flag_i = sb("flag_i", [1, 1], I32)
        iota_i = sb("iota_i", [P, SW], I32)
        iota = sb("iota", [P, SW])
        ident = sb("ident", [P, P])
        w_c = sb("w_c", [F, 2, F])
        w_g = sb("w_g", [F, 2, F])
        we_blk = sb("we_blk", [P, G * F])
        bias_b = sb("bias_b", [PN, 3, F])
        colv = sb("colv", [F, 4])
        deg = sb("deg", [PN, J])
        dinv = sb("dinv", [PN, J])
        stat = sb("stat", [PN, J, 6])
        mean = sb("mean", [PN, J])
        rstd = sb("rstd", [PN, J])
        root_in = sb("root_in", [PN, J])
        root_out = sb("root_out", [PN, J])
        tmp_j = sb("tmp_j", [PN, J])
        degT = sb("degT", [P, CA, AL])
        idx = [sb(f"idx{u}", [P, G], I32) for u in range(U)]
        attr = [sb(f"attr{u}", [P, 3 * G]) for u in range(U)]
        rows_g = [sb(f"rows_g{u}", [P, G * F]) for u in range(U)]
        hot = [sb(f"hot{u}", [P, G, W]) for u in range(U)]
        ea = [sb(f"ea{u}", [P, G * KE]) for u in range(U)]
        eaT = sb("eaT", [P, U * P])
        hot_b = [sb(f"hot_b{k}", [P, U * G, AL]) for k in range(2)]
        hot_a = [sb(f"hot_a{k}", [P, U * G, WA]) for k in range(2)]
        far = sb("far", [P, G, SW])
        far_i = sb("far_i", [P, 3, G], I32)
        far_c = sb("far_c", [P, 2, G])
        z1 = [far[0:F, k, :] for k in range(2)]
        bn = sb("bn", [F, NW, 6])
        bnv = sb("bnv", [F, 8])

        bank = [ctx.enter_context(nc.psum_tensor(f"bank{k}", [P, 512], F32)) for k in range(8)]
        ps_agg = [bank[u][0:F, 0:W] for u in range(U)]
        ps_e = [bank[3 + u][:, 0:G * F] for u in range(U)]
        ps_t = bank[6][:, 0:U * P]
        ps_far = bank[7][0:F, 0:SW]
        ps_deg = bank[7][0:AL, 0:NA + WA]

        s_dst, s_src, s_wgt = sem("dst_loaded"), sem("src_loaded"), sem("weight_loaded")
        s_x, s_par, s_blk = sem("x_loaded"), sem("params_loaded"), sem("we_loaded")
        s_const, s_blk0, s_zero = sem("constants_made"), sem("we_cleared"), sem("far_cleared")
        s_v = sem("vector_step")
        s_rows, s_tr, s_trc = sem("rows_ready"), sem("edges_transposed"), sem("edges_copied")
        s_wt, s_flag = sem("windows_transposed"), sem("flag_ready")
        s_dhot, s_dsum, s_dall = sem("deg_hot_ready"), sem("deg_hot_used"), sem("deg_summed")
        s_dha, s_far0 = sem("deg_hot_a"), sem("far_zero_again")
        s_dsb, s_dT, s_dc = sem("deg_in_sbuf"), sem("deg_transposed"), sem("deg_copied")
        s_dout, s_din = sem("deg_stored"), sem("deg_loaded")
        s_root, s_rooted = sem("root_wanted"), sem("root_done")
        s_tab, s_tabw = sem("table_chunk_ready"), sem("table_stored")
        s_nt, s_ntc = sem("nodes_transposed"), sem("nodes_copied")
        s_lin, s_linv, s_relu = sem("linear_done"), sem("linear_read"), sem("layer1_relu")
        s_h2 = sem("gin_input_ready")
        s_exp, s_expd, s_ln, s_lnd = sem("exp_wanted"), sem("exp_done"), sem("log_wanted"), sem("log_done")
        s_m1, s_z1, s_m2, s_z2 = sem("mlp1_done"), sem("mlp1_relu"), sem("mlp2_done"), sem("mlp2_biased")
        s_bn, s_y = sem("bn_ready"), sem("bn_applied")
        s_yt, s_ya, s_out = sem("out_transposed"), sem("out_ready"), sem("out_stored")

        class Ring:

            def __init__(self, name, slots):
                self.slots = slots
                self.staged = sem(f"{name}_staged")
                self.issue = sem(f"{name}_issue")
                self.hot = sem(f"{name}_hot")
                self.agg = sem(f"{name}_agg")
                self.added = sem(f"{name}_added")
                self.ea = [sem(f"{name}_ea{u}") for u in range(slots)]
                self.tr = sem(f"{name}_ea_transposed")
                self.trc = sem(f"{name}_ea_copied")
                self.lin = sem(f"{name}_ea_linear")
                self.msg = sem(f"{name}_msg")
                self.relu = sem(f"{name}_relu")

        fast, slow = Ring("fast", U), Ring("slow", 1)
        fast_got = [sem(f"fast_gathered{u}") for u in range(U)]
        slow_got = [sem(f"slow_gathered{p}") for p in range(PASSES)]
        far_used = sem("far_used")
        far_moved = sem("far_moved")
        far_deg = sem("far_deg_step")
        far_dsum = sem("far_deg_used")
        USES = [ITERS + 1] + [ITERS] * (U - 1)

        def each_group(eng, body):
            with eng.Fori(0, ITERS) as it:
                for u in range(U):
                    body(it * U + u, it, u, P)
            body(FULL, ITERS, 0, TP)

        def if_far(eng, sweep):
            any_far = eng.value_load(flag_i[0:1, 0:1], min_val=0, max_val=1)
            with eng.If(any_far > 0):
                sweep()

        def each_slow(eng, body):
            with eng.Fori(0, FULL) as s:
                body(s, P)
            body(FULL, TP)

        def by_group(t, s):
            return t[:, bass.ds(s, 1), :].rearrange("p s k -> p (s k)")

        block = ctx.enter_context(nc.Block())

        @block.sync
        def _(sp):
            def load_rows(tile, dram, s):
                q = CH - 1
                n = q * P * GE
                end = FULL * GE
                sp.dma_start(tile[:, 0:q, :], dram[0:n].rearrange("(c q e) -> q c e", q=P, e=GE)).then_inc(s, 16)
                sp.dma_start(tile[0:LASTQ - 1, q, :], dram[n:end].rearrange("(q e) -> q e", e=GE)).then_inc(s, 16)
                sp.dma_start(tile[LASTQ - 1:LASTQ, q, 0:G * TP],
                             dram[end:E].rearrange("(a e) -> a e", a=1)).then_inc(s, 16)
                sp.dma_start(tile[LASTQ - 1:LASTQ, q, G * TP:GE],
                             dram[E - (GE - G * TP):E].rearrange("(a e) -> a e", a=1)).then_inc(s, 16)

            def node_dma(to_dram, dram, tile, c0, c1, s):
                d = dram.rearrange("(p j) f -> p j f", j=J)
                for a, b in ((0, PK), (PK, PN)):
                    there, here = d[a:b, c0:c1, :], tile[a:b, c0:c1, :]
                    sp.dma_start(*((there, here) if to_dram else (here, there))).then_inc(s, 16)

            load_rows(dst_i, dst, s_dst)
            load_rows(src_i, src, s_src)
            load_rows(row_wgt, edge_weight, s_wgt)
            node_dma(False, x, x_sb, 0, J, s_x)
            for t, w in ((w_c[:, 0, :], c1_w), (w_c[:, 1, :], c2_w), (w_g[:, 0, :], g1_w), (w_g[:, 1, :], g2_w)):
                sp.dma_start(t, w).then_inc(s_par, 16)
            for k, b in enumerate((c1_b, c2_b, be)):
                sp.dma_start(bias_b[:, k, :], b.rearrange("(a n) -> a n", a=1).to_broadcast([PN, F])).then_inc(s_par, 16)
            for k, b in enumerate((g1_b, g2_b, gamma, beta)):
                sp.dma_start(colv[:, k:k + 1], b.rearrange("(n a) -> n a", a=1)).then_inc(s_par, 16)
            sp.wait_ge(s_blk0, 1)
            for g in range(G):
                sp.dma_start(we_blk[KE * g:KE * g + KE, F * g:F * g + F], we).then_inc(s_blk, 16)

            sp.wait_ge(s_dc, CA)
            for c in range(CA):
                n = min(P, NA - c * P)
                sp.dma_start(deg_lin[c * P * AL:(c * P + n) * AL].rearrange("(q b) -> q b", b=AL),
                             degT[0:n, c, :]).then_inc(s_dout, 16)
            sp.wait_ge(s_dout, 16 * CA)
            sp.dma_start(deg[:, :], deg_lin[0:N].rearrange("(p j) -> p j", j=J)).then_inc(s_din, 16)

            for p in range(PASSES):
                for c in range(NC):
                    if p == 1:
                        sp.wait_ge(s_relu, (c + 1) * JC)
                    else:
                        sp.wait_ge(s_tab, (p // 2) * NC + c + 1)
                    node_dma(True, table[p], tab, c * JC, (c + 1) * JC, s_tabw)

            def load_ea(ring, s, u, np_):
                sp.wait_ge(ring.tr, s + 1)
                sp.dma_start(ea[u][0:np_, :],
                             edge_attr[bass.ds(s * GE, G * np_), :].rearrange("(p g) k -> p (g k)", g=G)
                             ).then_inc(ring.ea[u], 16)

            each_group(sp, lambda s, it, u, np_: load_ea(fast, s, u, np_))

            def sweep():
                sp.wait_ge(fast.tr, NS + U)
                each_slow(sp, lambda s, np_: load_ea(slow, s, 0, np_))

            if_far(sp, sweep)

            for c in range(NC):
                sp.wait_ge(s_ya, (c + 1) * QC)
                node_dma(True, out, x_sb, c * JC, (c + 1) * JC, s_out)
            sp.wait_ge(s_out, 32 * NC)

        @block.gpsimd
        def _(pool):
            pool.memset(we_blk[:, :], 0.0).then_inc(s_blk0, 1)
            pool.iota(iota_i[:, :], pattern=[[1, SW]], base=0, channel_multiplier=0).then_inc(s_const, 1)
            pool.memset(ident[:, :], 0.0).then_inc(s_const, 1)
            pool.wait_ge(s_const, 2)
            pool.affine_select(out=ident[:, :], in_=ident[:, :], compare_op=ALU.not_equal, fill=1.0,
                               base=0, pattern=[[-1, P]], channel_multiplier=1).then_inc(s_const, 1)

            def gather(ring, p, s, u, np_, got):
                pool.wait_ge(ring.staged, p * NS + s + 1)
                pool.sem_inc(ring.issue, 1)
                for g in range(G):
                    pool.indirect_dma_start(
                        out=rows_g[u][0:np_, g * F:(g + 1) * F], out_offset=None, in_=table[p],
                        in_offset=bass.IndirectOffsetOnAxis(ap=idx[u][0:np_, g:g + 1], axis=0),
                    ).then_inc(got, 16)

            for p in range(PASSES):
                pool.wait_ge(s_tabw, 32 * NC * (p + 1))
                each_group(pool, lambda s, it, u, np_: gather(fast, p, s, u, np_, fast_got[u]))
                if_far(pool, lambda: each_slow(pool, lambda s, np_: gather(slow, p, s, 0, np_, slow_got[p])))

        @block.scalar
        def _(act):
            act.sem_inc(fast.trc, U)
            act.sem_inc(slow.trc, 1)

            for n in range(4 * CH):
                c, k = divmod(n, 4)
                nq = P if c < CH - 1 else LASTQ
                act.wait_ge(s_tr, n + 1)
                act.activation(edge[:, c * P:c * P + nq, k * G:(k + 1) * G],
                               bank[n % 2][:, 0:G * nq].rearrange("p (g q) -> p q g", g=G),
                               ACT.Copy).then_inc(s_trc, 1)

            def root(n, o, i):
                act.wait_ge(s_root, n + 1)
                act.activation(o, i, ACT.Sqrt).then_inc(s_rooted, 1)

            def copy_nodes(p, q):
                act.wait_ge(s_nt, p * NQ + q + 1)
                act.activation(acc_j[:, q * JQ:(q + 1) * JQ, :],
                               bank[3 + q % 2][0:F, 0:JQ * PN].rearrange("f (j p) -> f j p", j=JQ),
                               ACT.Copy).then_inc(s_ntc, 1)

            def stage(ring, p, s, u, np_):
                e = by_group(edge[0:np_, :, :], s)
                act.activation(attr[u][0:np_, :], e[:, G:4 * G], ACT.Copy)
                act.activation(idx[u][0:np_, :], e[:, 0:G], ACT.Copy).then_inc(ring.staged, 1)

            def stage_fast(p, s, u, np_):
                act.wait_ge(fast.agg, p * NS + s + 1)
                stage(fast, p, s, u, np_)

            def stage_slow(p, s, np_):
                act.wait_ge(slow.added, (p * NS + s) * NW + 1)
                stage(slow, p, s, 0, np_)

            def copy_eaT(ring, s, k, np_):
                act.wait_ge(ring.tr, s + k + ring.slots)
                act.wait_ge(ring.lin, s + ring.slots)
                w = (k - 1) * P + np_
                act.activation(eaT[:, 0:w], ps_t[:, 0:w], ACT.Copy).then_inc(ring.trc, k)

            def relu_msg(ring, s, u, np_):
                act.wait_ge(ring.msg, s + 1 + ring.slots)
                act.activation(rows_g[u][0:np_, :], rows_g[u][0:np_, :], ACT.Relu).then_inc(ring.relu, 1)

            def sweep(p):
                def one(s, np_):
                    stage_slow(p, s, np_)
                    if p == 2:
                        copy_eaT(slow, s, 1, np_)
                        relu_msg(slow, s, 0, np_)
                act.wait_ge(fast.agg, U + (p + 1) * NS)
                each_slow(act, one)

            root(0, root_out[:, :], root_in[:, :])
            root(1, root_out[:, :], root_in[:, :])
            act.wait_ge(s_flag, 1)
            for q in range(NQ):
                copy_nodes(0, q)
            each_group(act, lambda s, it, u, np_: stage_fast(0, s, u, np_))
            if_far(act, lambda: sweep(0))

            LAG = 3
            for q in range(NQ + LAG):
                if q < NQ:
                    for j in range(q * JQ, (q + 1) * JQ):
                        act.wait_ge(s_linv, j + 1)
                        act.activation(tab[:, j, :], tab[:, j, :], ACT.Relu, scale=dinv[:, j:j + 1]).then_inc(s_relu, 1)
                if q >= LAG:
                    copy_nodes(1, q - LAG)
            act.wait_ge(fast.agg, U + NS)
            each_group(act, lambda s, it, u, np_: stage_fast(1, s, u, np_))
            if_far(act, lambda: sweep(1))

            for c in range(NC):
                act.wait_ge(s_exp, c + 1)
                ch = tab[:, c * JC:(c + 1) * JC, :]
                act.activation(ch, ch, ACT.Exp).then_inc(s_expd, 1)
            act.wait_ge(s_ln, 1)
            act.activation(root_out[:, :], root_in[:, :], ACT.Ln).then_inc(s_lnd, 1)
            root(2, root_out[:, :], root_in[:, :])
            for q in range(NQ):
                copy_nodes(2, q)

            act.wait_ge(fast.agg, U + 2 * NS)
            for u in range(U):
                stage_fast(2, u, u, P)

            def gin_body(s0, last):
                copy_eaT(fast, s0, U, P)
                for u in range(U):
                    relu_msg(fast, s0 + u, u, P)
                    if not last:
                        stage_fast(2, s0 + U + u, u, P)
                    elif u == 0:
                        stage_fast(2, FULL, 0, TP)

            with act.Fori(0, ITERS - 1) as it:
                gin_body(it * U, False)
            gin_body(FULL - U, True)
            copy_eaT(fast, FULL, 1, TP)
            relu_msg(fast, FULL, 0, TP)
            if_far(act, lambda: sweep(2))

            for w in range(NW):
                act.wait_ge(s_m1, w + 1)
                act.activation(z1[w % 2], bank[w % 2][0:F, 0:SW], ACT.Relu, bias=colv[:, 0:1]).then_inc(s_z1, 1)
                if w >= 1:
                    act.wait_ge(s_m2, w)
                    act.activation(acc[:, (w - 1) * SW:w * SW], bank[2 + (w - 1) % 2][0:F, 0:SW], ACT.Identity,
                                   bias=colv[:, 1:2]).then_inc(s_z2, 1)
            act.wait_ge(s_m2, NW)
            act.activation(acc[:, (NW - 1) * SW:N], bank[2 + (NW - 1) % 2][0:F, 0:SW], ACT.Identity,
                           bias=colv[:, 1:2]).then_inc(s_z2, 1)
            root(3, bnv[:, 3:4], bnv[:, 2:3])
            act.wait_ge(s_bn, 1)
            act.activation(acc[:, 0:N], acc[:, 0:N], ACT.Relu, scale=bnv[:, 6:7], bias=bnv[:, 7:8]).then_inc(s_y, 1)

        @block.tensor
        def _(pe):
            for r, n in ((fast, U), (slow, 1)):
                pe.sem_inc(r.agg, n)
                pe.sem_inc(r.tr, n)
                pe.sem_inc(r.lin, n)
            pe.sem_inc(far_used, 1)
            pe.sem_inc(far_dsum, 1)
            pe.sem_inc(s_dsum, 2)

            pe.wait_ge(s_const, 3)
            pe.wait_ge(s_rows, 1)
            pe.wait_ge(s_wgt, 64)
            for n in range(4 * CH):
                c, k = divmod(n, 4)
                nq = P if c < CH - 1 else LASTQ
                if n >= 2:
                    pe.wait_ge(s_trc, n - 1)
                for g in range(G):
                    last = pe.transpose(bank[n % 2][:, g * nq:(g + 1) * nq], row[k][0:nq, c, g:GE:G], ident[0:nq, 0:nq])
                last.then_inc(s_tr, 1)
            for c in range(CH):
                pe.transpose(bank[2][0:1, c * P:(c + 1) * P], win_f[:, c:c + 1], ident[:, :])
                last = pe.transpose(bank[3][0:1, c * P:(c + 1) * P], span_f[:, c:c + 1], ident[:, :])
            last.then_inc(s_wt, 1)

            pe.wait_ge(s_zero, 1)
            pe.matmul(ps_deg, far[:, 0, 0:AL], far[:, 1, 0:NA + WA], start=True, stop=False)
            pe.wait_ge(s_flag, 1)

            def deg_step(n, s0, k, ng, np_):
                pe.wait_ge(s_dhot, n + 1)
                for i in range(ng):
                    w0 = pe.value_load(win_row[0:1, bass.ds(s0 + i, 1)], min_val=0, max_val=NA - 1)
                    for g in range(G):
                        t = i * G + g
                        last = pe.matmul(bank[7][0:AL, bass.ds(w0, WA)], hot_b[k][0:np_, t, :], hot_a[k][0:np_, t, :],
                                         start=False, stop=False)
                last.then_inc(s_dsum, 1)

            with pe.Fori(0, ITERS // 2) as it:
                for k in range(2):
                    deg_step(it * 2 + k, it * 2 * U + k * U, k, U, P)
            deg_step(ITERS, FULL, 0, 1, TP)

            def deg_sweep():
                def one(s, np_):
                    pe.wait_ge(far_deg, 6 * s + 6)
                    for g in range(G):
                        last = pe.matmul(bank[7][0:AL, 0:NA], hot_b[0][0:np_, g, :], far[0:np_, g, 0:NA],
                                         start=False, stop=False)
                    last.then_inc(far_dsum, 1)
                each_slow(pe, one)

            if_far(pe, deg_sweep)
            pe.wait_ge(s_zero, 2)
            pe.matmul(ps_deg, hot_b[0][:, 0, :], far[:, 1, 0:NA + WA], start=False, stop=True).then_inc(s_dall, 1)
            pe.wait_ge(s_dsb, 1)
            for c in range(CA):
                n = min(P, NA - c * P)
                last = pe.transpose(bank[2][0:n, c * AL:(c + 1) * AL], deg_sb[:, c * P:c * P + n], ident[0:AL, 0:AL])
            last.then_inc(s_dT, 1)

            def transpose_nodes(p, q):
                if q >= 2:
                    pe.wait_ge(s_ntc, p * NQ + q - 1)
                for i in range(JQ):
                    last = pe.transpose(bank[3 + q % 2][0:F, i * PN:(i + 1) * PN], tab[:, q * JQ + i, :], ident[0:PN, 0:PN])
                last.then_inc(s_nt, 1)

            def transpose_ea(ring, s, first, it, u, np_):
                pe.wait_ge(ring.ea[u], 16 * (it + 1))
                pe.wait_ge(ring.trc, first + ring.slots)
                pe.transpose(ps_t[:, u * P:u * P + np_], ea[u][0:np_, :], ident[0:np_, 0:np_]).then_inc(ring.tr, 1)

            def linear_ea(ring, s, upto, u, np_):
                pe.wait_ge(ring.trc, upto + ring.slots)
                pe.wait_ge(ring.msg, s + 1)
                pe.matmul(ps_e[u][0:np_, :], eaT[:, u * P:u * P + np_], we_blk[:, :], start=True, stop=True).then_inc(ring.lin, 1)

            def aggregate(p, s, it, u, np_):
                n = p * NS + s
                pe.wait_ge(fast.hot, n + 1)
                pe.wait_ge(fast.added, n + 1)
                if p < 2:
                    pe.wait_ge(fast_got[u], 16 * G * (p * USES[u] + it + 1))
                else:
                    pe.wait_ge(fast.relu, s + 1)
                for g in range(G):
                    last = pe.matmul(ps_agg[u], rows_g[u][0:np_, g * F:(g + 1) * F], hot[u][0:np_, g, :],
                                     start=g == 0, stop=g == G - 1)
                last.then_inc(fast.agg, 1)

            def sweep(p):
                def one(s, np_):
                    n = p * NS + s
                    if p == 2:
                        transpose_ea(slow, s, s, s, 0, np_)
                        linear_ea(slow, s, s + 1, 0, np_)
                    with pe.Fori(0, NW) as w:
                        if p == 2:
                            pe.wait_ge(slow.relu, s + 1)
                        else:
                            pe.wait_ge(slow_got[p], 16 * G * (s + 1))
                        pe.wait_ge(slow.hot, n * NW + w + 1)
                        pe.wait_ge(slow.added, n * NW + w + 1)
                        for g in range(G):
                            last = pe.matmul(ps_far, rows_g[0][0:np_, g * F:(g + 1) * F], far[0:np_, g, :],
                                             start=g == 0, stop=g == G - 1)
                        last.then_inc(far_used, 1)
                each_slow(pe, one)
                pe.wait_ge(slow.added, (p + 1) * NS * NW + 1)

            def linear(p, q):
                if q >= 3:
                    pe.wait_ge(s_linv, p * J + (q - 2) * JQ)
                for i in range(JQ):
                    last = pe.matmul(bank[q % 3][0:PN, i * F:(i + 1) * F], acc_j[:, q * JQ + i, :], w_c[:, p, :],
                                     start=True, stop=True)
                last.then_inc(s_lin, 1)

            for c in range(NC):
                pe.wait_ge(s_tab, c + 1)
                for q in range(c * QC, (c + 1) * QC):
                    transpose_nodes(0, q)
            each_group(pe, lambda s, it, u, np_: aggregate(0, s, it, u, np_))
            pe.wait_ge(fast.added, U + NS)
            if_far(pe, lambda: sweep(0))

            pe.wait_ge(s_par, 16 * 11)
            LAG = 3
            for q in range(NQ + LAG):
                if q < NQ:
                    linear(0, q)
                if q >= LAG:
                    pe.wait_ge(s_relu, (q - LAG + 1) * JQ)
                    transpose_nodes(1, q - LAG)
            each_group(pe, lambda s, it, u, np_: aggregate(1, s, it, u, np_))
            pe.wait_ge(fast.added, U + 2 * NS)
            if_far(pe, lambda: sweep(1))

            for q in range(NQ):
                linear(1, q)
            for c in range(NC):
                pe.wait_ge(s_h2, c + 1)
                for q in range(c * QC, (c + 1) * QC):
                    transpose_nodes(2, q)

            pe.wait_ge(s_blk, 16 * G)
            def gin_body(s0, it):
                for u in range(U):
                    transpose_ea(fast, s0 + u, s0, it, u, P)
                for u in range(U):
                    linear_ea(fast, s0 + u, s0 + U, u, P)
                for u in range(U):
                    aggregate(2, s0 + u, it, u, P)
            with pe.Fori(0, ITERS) as it:
                gin_body(it * U, it)
            transpose_ea(fast, FULL, FULL, ITERS, 0, TP)
            linear_ea(fast, FULL, NS, 0, TP)
            aggregate(2, FULL, ITERS, 0, TP)
            pe.wait_ge(fast.added, U + 3 * NS)
            if_far(pe, lambda: sweep(2))

            for w in range(NW + 1):
                if w < NW:
                    if w >= 2:
                        pe.wait_ge(s_z1, w - 1)
                    pe.matmul(bank[w % 2][0:F, 0:SW], w_g[:, 0, :], acc[:, w * SW:(w + 1) * SW],
                              start=True, stop=True).then_inc(s_m1, 1)
                if w >= 1:
                    v = w - 1
                    pe.wait_ge(s_z1, w)
                    if v >= 2:
                        pe.wait_ge(s_z2, v - 1)
                    pe.matmul(bank[2 + v % 2][0:F, 0:SW], w_g[:, 1, :], z1[v % 2],
                              start=True, stop=True).then_inc(s_m2, 1)
            pe.wait_ge(s_y, 1)
            for q in range(NQ):
                if q >= 3:
                    pe.wait_ge(s_ya, q - 2)
                for i in range(JQ):
                    last = pe.transpose(bank[4 + q % 3][0:PN, i * F:(i + 1) * F], acc_j[:, q * JQ + i, :], ident[0:F, 0:F])
                last.then_inc(s_yt, 1)

        @block.vector
        def _(dve):
            for r, n in ((fast, U), (slow, 1)):
                dve.sem_inc(r.added, n)
                dve.sem_inc(r.msg, n)

            steps = [0]

            def then(ins):
                steps[0] += 1
                ins.then_inc(s_v, 1)
                dve.wait_ge(s_v, steps[0])

            def parts(f):
                f(slice(0, P), slice(0, CH - 1))
                return f(slice(0, LASTQ), slice(CH - 1, CH))

            dve.memset(acc_t[:, N:], 0.0)
            dve.memset(win_f[:, :], 0.0)
            then(dve.memset(span_f[:, :], 0.0))
            dve.memset(far[:, :, :], 0.0).then_inc(s_zero, 1)
            dve.wait_ge(s_const, 3)
            dve.tensor_copy(iota[:, :], iota_i[:, :])

            dve.wait_ge(s_dst, 64)
            then(parts(lambda q, c: dve.tensor_copy(row_dst[q, c, :], dst_i[q, c, :])))
            parts(lambda q, c: dve.tensor_reduce(least[q, c], row_dst[q, c, :], AX.X, ALU.min))
            then(parts(lambda q, c: dve.tensor_reduce(most[q, c], row_dst[q, c, :], AX.X, ALU.max)))
            then(parts(lambda q, c: dve.tensor_copy(base_i[q, c], least[q, c])))
            then(parts(lambda q, c: dve.tensor_single_scalar(win_i[q, c], base_i[q, c], 5, ALU.arith_shift_right)))
            then(parts(lambda q, c: dve.tensor_copy(win_f[q, c], win_i[q, c])))
            then(parts(lambda q, c: dve.tensor_scalar(base_f[q, c], win_f[q, c], float(AL), None, ALU.mult)))
            parts(lambda q, c: dve.tensor_tensor(span_f[q, c], most[q, c], base_f[q, c], ALU.subtract))
            for c in range(CH):
                q = slice(0, P if c < CH - 1 else LASTQ)
                last = dve.tensor_scalar(row_rel[q, c, :], row_dst[q, c, :], base_f[q, c:c + 1], None, ALU.subtract)
            then(last)
            then(parts(lambda q, c: dve.tensor_scalar(row_far[q, c, :], row_rel[q, c, :], float(W), FAR, ALU.is_lt, ALU.mult)))
            parts(lambda q, c: dve.tensor_tensor(row_far[q, c, :], row_far[q, c, :], row_dst[q, c, :], ALU.add))
            dve.wait_ge(s_src, 64)
            parts(lambda q, c: dve.tensor_copy(row_src[q, c, :], src_i[q, c, :])).then_inc(s_rows, 1)

            def ln_stats(c):
                for j in range(c * JC, (c + 1) * JC):
                    last = dve.bn_stats(stat[:, j, :], x_sb[:, j, :])
                return last

            def ln_rstd_start():
                me, mo, ve, vo = stat[:, :, 1], stat[:, :, 4], stat[:, :, 2], stat[:, :, 5]
                dve.tensor_tensor(mean[:, :], me, mo, ALU.add)
                dve.tensor_tensor(tmp_j[:, :], me, mo, ALU.subtract)
                then(dve.tensor_tensor(root_in[:, :], ve, vo, ALU.add))
                dve.tensor_scalar(mean[:, :], mean[:, :], 0.5, None, ALU.mult)
                then(dve.tensor_tensor(tmp_j[:, :], tmp_j[:, :], tmp_j[:, :], ALU.mult))
                then(dve.tensor_scalar(root_in[:, :], root_in[:, :], 1.0 / F, EPS, ALU.mult, ALU.add))
                then(dve.scalar_tensor_tensor(root_in[:, :], tmp_j[:, :], 0.25, root_in[:, :], ALU.mult, ALU.add))
                dve.sem_inc(s_root, 1)

            dve.wait_ge(s_x, 32)
            for c in range(NC):
                last = ln_stats(c)
            then(last)
            ln_rstd_start()

            dve.wait_ge(s_wt, 1)
            dve.tensor_copy(win_row[0:1, :], bank[2][0:1, 0:CH * P])
            then(dve.tensor_reduce(flag_f[0:1, :], bank[3][0:1, 0:CH * P], AX.X, ALU.max))
            dve.tensor_scalar(flag_i[0:1, :], flag_f[0:1, :], float(W), None, ALU.is_ge).then_inc(s_flag, 1)

            dve.wait_ge(s_trc, 4 * CH)
            v3 = lambda t: t.rearrange("p (s g) -> p s g", g=G)
            then(dve.tensor_copy(v3(col_i), edge[:, :, G:2 * G]))
            then(dve.tensor_single_scalar(col_i2, col_i, AL - 1, ALU.bitwise_and))
            dve.tensor_copy(col_b, col_i2)
            then(dve.tensor_single_scalar(col_i, col_i, 5, ALU.arith_shift_right))
            then(dve.tensor_copy(col_a, col_i))

            def deg_hot(n, s0, k, ng, np_):
                t = ng * G
                cols = lambda a: a[0:np_, bass.ds(s0 * G, t)].unsqueeze(2)
                dve.wait_ge(s_dsum, n + 1)
                ib = iota[0:np_, 0:AL].unsqueeze(1).to_broadcast([np_, t, AL])
                ia = iota[0:np_, 0:WA].unsqueeze(1).to_broadcast([np_, t, WA])
                a3 = hot_a[k][0:np_, 0:t, :]
                dve.tensor_tensor(a3, ia, cols(col_a).to_broadcast([np_, t, WA]), ALU.is_equal).then_inc(s_dha, 1)
                dve.tensor_tensor(hot_b[k][0:np_, 0:t, :], ib, cols(col_b).to_broadcast([np_, t, AL]), ALU.is_equal)
                wgt = edge[0:np_, bass.ds(s0, ng), 2 * G:3 * G].unsqueeze(3).to_broadcast([np_, ng, G, WA])
                a4 = a3.rearrange("p (s g) a -> p s g a", g=G)
                dve.wait_ge(s_dha, n + 1)
                dve.tensor_tensor(a4, a4, wgt, ALU.mult).then_inc(s_dhot, 1)

            with dve.Fori(0, ITERS // 2) as it:
                for k in range(2):
                    deg_hot(it * 2 + k, it * 2 * U + k * U, k, U, P)
            deg_hot(ITERS, FULL, 0, 1, TP)

            def deg_sweep():
                dve.wait_ge(s_dsum, ITERS + 3)
                def one(s, np_):
                    k = 6 * s
                    o = slice(0, np_)
                    dve.wait_ge(far_dsum, s + 1)
                    dve.tensor_copy(far_i[o, 0, :], by_group(edge[o, :, :], s)[:, 3 * G:4 * G]).then_inc(far_deg, 1)
                    dve.wait_ge(far_deg, k + 1)
                    dve.tensor_single_scalar(far_i[o, 1, :], far_i[o, 0, :], AL - 1, ALU.bitwise_and).then_inc(far_deg, 1)
                    dve.tensor_single_scalar(far_i[o, 2, :], far_i[o, 0, :], 5, ALU.arith_shift_right).then_inc(far_deg, 1)
                    dve.wait_ge(far_deg, k + 3)
                    dve.tensor_copy(far_c[o, :, :], far_i[o, 1:3, :]).then_inc(far_deg, 1)
                    dve.tensor_copy(attr[0][o, 0:G], by_group(edge[o, :, :], s)[:, 2 * G:3 * G]).then_inc(far_deg, 1)
                    dve.wait_ge(far_deg, k + 5)
                    for g in range(G):
                        dve.tensor_scalar(hot_b[0][o, g, :], iota[o, 0:AL], far_c[o, 0, g:g + 1], None, ALU.is_equal)
                        last = dve.tensor_scalar(far[o, g, 0:NA], iota[o, 0:NA], far_c[o, 1, g:g + 1],
                                                 attr[0][o, g:g + 1], ALU.is_equal, ALU.mult)
                    last.then_inc(far_deg, 1)
                each_slow(dve, one)
                dve.wait_ge(far_dsum, NS + 1)
                dve.memset(far[:, 1, :], 0.0).then_inc(s_far0, 1)
                dve.wait_ge(s_far0, 1)

            if_far(dve, deg_sweep)
            dve.wait_ge(s_dsum, ITERS + 3)
            dve.memset(hot_b[0][:, 0, :], 0.0).then_inc(s_zero, 1)
            dve.wait_ge(s_dall, 1)
            dve.tensor_copy(deg_sb, bank[7][0:AL, 0:NA]).then_inc(s_dsb, 1)
            dve.wait_ge(s_dT, 1)
            for c in range(CA):
                n = min(P, NA - c * P)
                dve.tensor_copy(degT[0:n, c, :], bank[2][0:n, c * AL:(c + 1) * AL]).then_inc(s_dc, 1)
            dve.wait_ge(s_rooted, 1)
            then(dve.reciprocal(rstd[:, :], root_out[:, :]))
            dve.wait_ge(s_din, 16)
            then(dve.tensor_scalar(deg[:, :], deg[:, :], 1.0, None, ALU.add))
            then(dve.tensor_scalar(root_in[:, :], deg[:, :], TINY, None, ALU.max))
            dve.sem_inc(s_root, 1)
            dve.tensor_scalar(tmp_j[:, :], deg[:, :], 0.0, None, ALU.is_gt)
            dve.wait_ge(s_rooted, 2)
            then(dve.reciprocal(dinv[:, :], root_out[:, :]))
            then(dve.tensor_tensor(dinv[:, :], dinv[:, :], tmp_j[:, :], ALU.mult))
            then(dve.tensor_tensor(tmp_j[:, :], dinv[:, :], rstd[:, :], ALU.mult))

            def chunk(t, c):
                return t[:, c * JC:(c + 1) * JC, :]

            def bc(t, c):
                return t[:, c * JC:(c + 1) * JC].unsqueeze(2).to_broadcast([PN, JC, F])

            dve.wait_ge(s_tr, 4 * CH)
            for c in range(NC):
                then(dve.tensor_tensor(chunk(tab, c), chunk(x_sb, c), bc(mean, c), ALU.subtract))
                dve.scalar_tensor_tensor(chunk(tab, c), chunk(tab, c), 0.0, bc(tmp_j, c), ALU.max, ALU.mult).then_inc(s_tab, 1)

            def windows(it):
                return [dve.value_load(win_row[0:1, bass.ds(it * U + u, 1)], min_val=0, max_val=NA - 1) for u in range(U)]

            def build_hot(p, s, u, np_):
                dve.wait_ge(fast.staged, p * NS + s + 1)
                for g in range(G):
                    rel = attr[u][0:np_, g:g + 1]
                    if p < 2:
                        last = dve.tensor_scalar(hot[u][0:np_, g, :], iota[0:np_, 0:W], rel,
                                                 attr[u][0:np_, G + g:G + g + 1], ALU.is_equal, ALU.mult)
                    else:
                        last = dve.tensor_scalar(hot[u][0:np_, g, :], iota[0:np_, 0:W], rel, None, ALU.is_equal)
                last.then_inc(fast.hot, 1)

            def add_window(p, s, u, w0):
                n = p * NS + s
                dve.wait_ge(fast.agg, n + 1 + U)
                dve.wait_ge(fast.added, n + U)
                a = acc[:, bass.ds(w0 * AL, W)]
                dve.tensor_tensor(a, a, ps_agg[u], ALU.add).then_inc(fast.added, 1)

            def add_edge_term(ring, s, it, u, np_):
                dve.wait_ge(ring.lin, s + 1 + ring.slots)
                if ring is fast:
                    dve.wait_ge(fast_got[u], 16 * G * (2 * USES[u] + it + 1))
                else:
                    dve.wait_ge(slow_got[2], 16 * G * (s + 1))
                r = rows_g[u][0:np_, :]
                dve.tensor_tensor(r, r, ps_e[u][0:np_, :], ALU.add).then_inc(ring.msg, 1)

            def fast_pass(p):
                def body(it, us, np_, w):
                    s0 = it * U if us > 1 else FULL
                    for u in range(us):
                        build_hot(p, s0 + u, u, np_)
                    for u in range(us):
                        if p == 2:
                            add_edge_term(fast, s0 + u, it, u, np_)
                            if u >= 1:
                                add_window(p, s0 + u - 1, u - 1, w[u - 1])
                        else:
                            add_window(p, s0 + u, u, w[u])
                    if p == 2:
                        add_window(p, s0 + us - 1, us - 1, w[us - 1])
                dve.wait_ge(s_ntc, (p + 1) * NQ)
                with dve.Fori(0, ITERS) as it:
                    body(it, U, P, windows(it))
                w = dve.value_load(win_row[0:1, FULL:FULL + 1], min_val=0, max_val=NA - 1)
                body(ITERS, 1, TP, [w])

            def sweep(p):
                def one(s, np_):
                    n = p * NS + s
                    o = slice(0, np_)
                    if p == 2:
                        add_edge_term(slow, s, s, 0, np_)
                    with dve.Fori(0, NW) as w:
                        m = n * NW + w
                        dve.wait_ge(slow.staged, n + 1)
                        dve.wait_ge(far_used, m + 1)
                        dve.wait_ge(far_moved, m + 1)
                        for g in range(G):
                            tgt = attr[0][o, 2 * G + g:2 * G + g + 1]
                            if p < 2:
                                last = dve.tensor_scalar(far[o, g, :], iota[o, :], tgt, attr[0][o, G + g:G + g + 1],
                                                         ALU.is_equal, ALU.mult)
                            else:
                                last = dve.tensor_scalar(far[o, g, :], iota[o, :], tgt, None, ALU.is_equal)
                        last.then_inc(slow.hot, 1)
                        dve.wait_ge(slow.hot, m + 1)
                        t = attr[0][o, 2 * G:3 * G]
                        dve.tensor_scalar(t, t, -float(SW), None, ALU.add).then_inc(far_moved, 1)
                        dve.wait_ge(far_used, m + 2)
                        dve.wait_ge(slow.added, m + 1)
                        a = acc[:, bass.ds(w * SW, SW)]
                        dve.tensor_tensor(a, a, ps_far, ALU.add).then_inc(slow.added, 1)
                dve.wait_ge(fast.added, U + (p + 1) * NS)
                if p == 0:
                    dve.sem_inc(far_moved, 1)
                each_slow(dve, one)

            def linear_read(p, q):
                dve.wait_ge(s_lin, p * NQ + q + 1)
                for i in range(JQ):
                    j = q * JQ + i
                    last = dve.scalar_tensor_tensor(tab[:, j, :], bank[q % 3][0:PN, i * F:(i + 1) * F], dinv[:, j:j + 1],
                                                    bias_b[:, p, :], ALU.mult, ALU.add).then_inc(s_linv, 1)

            fast_pass(0)
            if_far(dve, lambda: sweep(0))
            dve.wait_ge(s_par, 16 * 11)
            dve.wait_ge(s_tabw, 32 * NC)
            for q in range(NQ):
                linear_read(0, q)
            fast_pass(1)
            if_far(dve, lambda: sweep(1))

            dve.wait_ge(s_tabw, 2 * 32 * NC)
            for c in range(NC):
                for q in range(c * QC, (c + 1) * QC):
                    linear_read(1, q)
                dve.wait_ge(s_linv, J + (c + 1) * JC)
                then(dve.tensor_reduce(root_in[:, c * JC:(c + 1) * JC], chunk(tab, c), AX.X, ALU.max))
                then(dve.tensor_tensor(chunk(tab, c), chunk(tab, c), bc(root_in, c), ALU.subtract))
                dve.tensor_tensor(chunk(x_sb, c), chunk(x_sb, c), chunk(tab, c), ALU.add).then_inc(s_exp, 1)
            for c in range(NC):
                dve.wait_ge(s_expd, c + 1)
                last = dve.tensor_reduce(root_in[:, c * JC:(c + 1) * JC], chunk(tab, c), AX.X, ALU.add)
            last.then_inc(s_ln, 1)
            dve.wait_ge(s_lnd, 1)
            for c in range(NC):
                then(dve.tensor_tensor(chunk(x_sb, c), chunk(x_sb, c), bc(root_out, c), ALU.subtract))
                last = ln_stats(c)
            then(last)
            ln_rstd_start()
            dve.wait_ge(s_rooted, 3)
            then(dve.reciprocal(rstd[:, :], root_out[:, :]))
            for c in range(NC):
                then(dve.tensor_tensor(chunk(tab, c), chunk(x_sb, c), bc(mean, c), ALU.subtract))
                dve.scalar_tensor_tensor(chunk(tab, c), chunk(tab, c), 0.0, bc(rstd, c), ALU.max, ALU.mult).then_inc(s_h2, 1)
            for c in range(NC):
                dve.wait_ge(s_nt, 2 * NQ + (c + 1) * QC)
                dve.tensor_tensor(chunk(tab, c), chunk(tab, c), bias_b[:, 2, :].unsqueeze(1).to_broadcast([PN, JC, F]),
                                  ALU.add).then_inc(s_tab, 1)
            fast_pass(2)
            if_far(dve, lambda: sweep(2))

            for w in range(NW):
                dve.wait_ge(s_z2, w + 1)
                last = dve.bn_stats(bn[:, w, :], acc[:, w * SW:(w + 1) * SW])
            then(last)
            then(dve.bn_aggr(bnv[:, 0:2], bn[:, :, :].rearrange("f w k -> f (w k)")))
            dve.tensor_scalar(bnv[:, 2:3], bnv[:, 1:2], EPS, None, ALU.add).then_inc(s_root, 1)
            dve.wait_ge(s_rooted, 4)
            then(dve.reciprocal(bnv[:, 4:5], bnv[:, 3:4]))
            then(dve.tensor_tensor(bnv[:, 6:7], bnv[:, 4:5], colv[:, 2:3], ALU.mult))
            then(dve.tensor_tensor(bnv[:, 5:6], bnv[:, 0:1], bnv[:, 6:7], ALU.mult))
            dve.tensor_tensor(bnv[:, 7:8], colv[:, 3:4], bnv[:, 5:6], ALU.subtract).then_inc(s_bn, 1)
            for q in range(NQ):
                dve.wait_ge(s_yt, q + 1)
                xs = x_sb[:, q * JQ:(q + 1) * JQ, :]
                dve.tensor_tensor(xs, xs, bank[4 + q % 3][0:PN, 0:JQ * F].rearrange("p (j f) -> p j f", j=JQ),
                                  ALU.add).then_inc(s_ya, 1)


_INS = ['x', 'src', 'dst', 'edge_attr_32', 'edge_weight', 'L0_gnn_W1', 'L0_gnn_b1', 'L0_gnn_W2', 'L0_gnn_b2',
        'L1_gnn_We', 'L1_gnn_be', 'L1_gnn_W1', 'L1_gnn_b1', 'L1_gnn_W2', 'L1_gnn_b2', 'L1_gnn_gamma', 'L1_gnn_beta']


def kernel(**inputs):
    import numpy as _np
    import concourse.bacc as _bacc
    from concourse import mybir as _mybir
    from concourse.bass_utils import run_bass_kernel_spmd as _run

    nc = _bacc.Bacc("TRN2", target_bir_lowering=False, num_devices=1)
    arrays, args = {}, []
    for name in _INS:
        a = _np.ascontiguousarray(inputs[name])
        arrays[f"in_{name}_dram"] = a
        args.append(nc.dram_tensor(f"in_{name}_dram", a.shape, _mybir.dt.from_np(a.dtype), kind="ExternalInput").ap())
    out = nc.dram_tensor("out_0_dram", inputs["x"].shape, _mybir.dt.float32, kind="ExternalOutput").ap()
    build_gnn(nc, *args, out)
    r = _run(nc, [arrays], core_ids=[0])
    return r.results[0]["out_0_dram"]
```

```python
import concourse.bass as bass
from concourse import mybir
from contextlib import ExitStack

F32 = mybir.dt.float32
I32 = mybir.dt.int32
BF16 = mybir.dt.bfloat16
ALU = mybir.AluOpType
ACT = mybir.ActivationFunctionType
AX = mybir.AxisListType


def build_gnn(nc, x, src, dst, edge_attr, edge_weight, c1_w, c1_b, c2_w, c2_b,
              we, be, g1_w, g1_b, g2_w, g2_b, gamma, beta, out):
    N, F = x.shape
    E = src.shape[0]
    KE = edge_attr.shape[1]
    P = 128
    G = 4
    GE = G * P
    NS = -(-E // GE)
    FULL = E // GE
    TP = (E - FULL * GE) // G
    U = 3
    ITERS = FULL // U
    DG = 5
    CH = -(-NS // P)
    LASTQ = NS - (CH - 1) * P
    W = 128
    AL = 32
    WA = W // AL
    NA = -(-N // AL)
    BK = 512
    NB = 3
    BA = -(-NA // NB)
    CA = -(-NA // P)
    J = 100
    PN = N // J
    PK = PN // 16 * 16
    JC = 20
    NC = J // JC
    JQ = 4
    NQ = J // JQ
    QC = JC // JQ
    SW = 500
    NW = N // SW
    FAR = -float(1 << 20)
    EPS = 1e-5
    TINY = 1.2e-38
    PASSES = 3
    assert FULL == NS - 1 and FULL % U == 0 and FULL % (2 * DG) == 0 and TP * G == E - FULL * GE and TP % 16 == 0
    assert N % J == 0 and N % SW == 0 and J % JC == 0 and JC % JQ == 0 and NA <= BK and NB * (BA + WA) <= BK

    table = [nc.dram_tensor(f"table{p}", (N, F), F32).ap() for p in range(PASSES)]
    deg_lin = nc.dram_tensor("deg_lin", (NA * AL,), F32).ap()

    ctx = ExitStack()
    with ctx:
        def sb(name, shape, dt=F32):
            return ctx.enter_context(nc.sbuf_tensor(name, shape, dt))

        def sem(name):
            return ctx.enter_context(nc.semaphore(name))

        x_sb = sb("x_sb", [PN, J, F])
        tab_t = sb("tab", [P, J * F])
        tab = tab_t[0:PN, :].rearrange("p (j f) -> p j f", j=J)
        acc_t = sb("acc", [P, N + W])
        acc = acc_t[0:F, :]
        acc_j = acc[:, 0:N].rearrange("f (p j) -> f j p", j=J)
        edge = sb("edge", [P, NS, 4 * G])
        part = lambda t, k, n: t[:, k * n:(k + 1) * n]
        row = [part(tab_t, k, CH * GE).rearrange("q (c e) -> q c e", c=CH) for k in range(4)]
        row_src, row_rel, row_wgt, row_far = row
        dst_i = part(acc_t, 0, CH * GE).bitcast(I32).rearrange("q (c e) -> q c e", c=CH)
        src_i = part(acc_t, 1, CH * GE).bitcast(I32).rearrange("q (c e) -> q c e", c=CH)
        row_dst = part(acc_t, 2, CH * GE).rearrange("q (c e) -> q c e", c=CH)
        off = 3 * CH * GE
        col_b = acc_t[:, off:off + NS * G]
        col_a = acc_t[:, off + NS * G:off + 2 * NS * G]
        col_i = part(acc_t, 1, NS * G).bitcast(I32)
        col_i2 = part(acc_t, 2, NS * G).bitcast(I32)
        deg_sb = part(acc_t, 2, NS * G)[0:AL, 0:NB * BA + WA]
        deg_k = part(acc_t, 1, NS * G)[0:AL, 0:NB * (BA + WA)]
        off2 = off + 2 * NS * G
        wgt3 = acc_t[:, off2:off2 + NB * NS * G // 2].bitcast(BF16).rearrange("p (t k) -> p t k", k=NB)
        wgt_r = acc_t[:, 0:NS * G]
        least = sb("least", [P, CH])
        most = sb("most", [P, CH])
        win_i = sb("win_i", [P, CH], I32)
        base_i = sb("base_i", [P, CH], I32)
        win_f = sb("win_f", [P, CH])
        base_f = sb("base_f", [P, CH])
        span_f = sb("span_f", [P, CH])
        win_row = sb("win_row", [1, CH * P], I32)
        bank_row = sb("bank_row", [1, CH * P], I32)
        row_f = sb("row_f", [1, 3, CH * P])
        flag_f = sb("flag_f", [1, 1])
        flag_i = sb("flag_i", [1, 1], I32)
        iota_i = sb("iota_i", [P, SW], I32)
        iota = sb("iota", [P, SW])
        ident = sb("ident", [P, P])
        w_c = sb("w_c", [F, 2, F])
        w_g = sb("w_g", [F, 2, F])
        we_blk = sb("we_blk", [P, G * F])
        bias_b = sb("bias_b", [PN, 3, F])
        colv = sb("colv", [F, 4])
        deg = sb("deg", [PN, J])
        dinv = sb("dinv", [PN, J])
        stat = sb("stat", [PN, J, 6])
        mean = sb("mean", [PN, J])
        rstd = sb("rstd", [PN, J])
        root_in = sb("root_in", [PN, J])
        root_out = sb("root_out", [PN, J])
        tmp_j = sb("tmp_j", [PN, J])
        nmax = sb("nmax", [PN, J])
        esum = sb("esum", [PN, J])
        logz = sb("logz", [PN, J])
        degT = sb("degT", [P, CA, AL])
        idx = [sb(f"idx{u}", [P, G], I32) for u in range(U)]
        attr = [sb(f"attr{u}", [P, 3 * G]) for u in range(U)]
        rows_g = [sb(f"rows_g{u}", [P, G * F]) for u in range(U)]
        hot = [sb(f"hot{u}", [P, G, W]) for u in range(U)]
        ea = [sb(f"ea{u}", [P, G * KE]) for u in range(U)]
        eaT = sb("eaT", [P, U * P])
        hot_b = [sb(f"hot_b{k}", [P, DG * G, AL], BF16) for k in range(2)]
        hot_a = [sb(f"hot_a{k}", [P, DG * G, WA], BF16) for k in range(2)]
        hot_w = [sb(f"hot_w{k}", [P, DG * G, WA, NB], BF16) for k in range(2)]
        zeros = sb("zeros", [P, 2 * NA], BF16)
        far = sb("far", [P, G, SW])
        far_i = sb("far_i", [P, 3, G], I32)
        far_c = sb("far_c", [P, 2, G])
        z1 = [far[0:F, k, :] for k in range(2)]
        bn = sb("bn", [F, NW, 6])
        bnv = sb("bnv", [F, 8])

        psum = ctx.enter_context(nc.psum_tensor("psum", [P, 8 * BK], F32))
        bank = [psum[:, k * BK:(k + 1) * BK] for k in range(8)]
        ps_agg = [bank[u][0:F, 0:W] for u in range(U)]
        ps_e = [bank[3 + u][:, 0:G * F] for u in range(U)]
        ps_t = bank[6][:, 0:U * P]
        ps_far = bank[7][0:F, 0:SW]
        ps_deg = psum[0:AL, 5 * BK:(5 + NB) * BK]
        ps_degf = bank[4][0:AL, 0:NA]

        s_dst, s_src, s_wgt = sem("dst_loaded"), sem("src_loaded"), sem("weight_loaded")
        s_x, s_par, s_blk = sem("x_loaded"), sem("params_loaded"), sem("we_loaded")
        s_const, s_blk0, s_zero = sem("constants_made"), sem("we_cleared"), sem("far_cleared")
        s_v = sem("vector_step")
        s_rows, s_tr, s_trc = sem("rows_ready"), sem("edges_transposed"), sem("edges_copied")
        s_wt, s_flag = sem("windows_transposed"), sem("flag_ready")
        s_dhot, s_dsum, s_dall = sem("deg_hot_ready"), sem("deg_hot_used"), sem("deg_summed")
        s_dha, s_w3, s_w3a = sem("deg_hot_a"), sem("weight_part_step"), sem("weight_parts_ready")
        s_dsb, s_dT, s_dc = sem("deg_in_sbuf"), sem("deg_transposed"), sem("deg_copied")
        s_dout, s_din = sem("deg_stored"), sem("deg_loaded")
        s_root, s_rooted = sem("root_wanted"), sem("root_done")
        s_tab, s_tabw = sem("table_chunk_ready"), sem("table_stored")
        s_nt, s_ntc = sem("nodes_transposed"), sem("nodes_copied")
        s_lin, s_linv, s_relu = sem("linear_done"), sem("linear_read"), sem("layer1_relu")
        s_relu_v = sem("layer1_relu_vector")
        s_exp, s_expd, s_ln, s_logz = sem("exp_wanted"), sem("exp_done"), sem("log_done"), sem("logz_ready")
        s_be = sem("gin_table_ready")
        s_mean, s_cent, s_x1 = sem("mean_ready"), sem("rows_centred"), sem("x_plus_gcn_ready")
        s_m1, s_z1, s_m2, s_z2 = sem("mlp1_done"), sem("mlp1_relu"), sem("mlp2_done"), sem("mlp2_biased")
        s_bn, s_y = sem("bn_ready"), sem("bn_applied")
        s_yt, s_ya, s_out = sem("out_transposed"), sem("out_ready"), sem("out_stored")

        class Ring:

            def __init__(self, name, slots):
                self.slots = slots
                self.staged = sem(f"{name}_staged")
                self.issue = sem(f"{name}_issue")
                self.hot = sem(f"{name}_hot")
                self.agg = sem(f"{name}_agg")
                self.added = sem(f"{name}_added")
                self.ea = [sem(f"{name}_ea{u}") for u in range(slots)]
                self.tr = sem(f"{name}_ea_transposed")
                self.trc = sem(f"{name}_ea_copied")
                self.lin = sem(f"{name}_ea_linear")
                self.msg = sem(f"{name}_msg")
                self.relu = sem(f"{name}_relu")

        fast, slow = Ring("fast", U), Ring("slow", 1)
        fast_got = [sem(f"fast_gathered{u}") for u in range(U)]
        slow_got = [sem(f"slow_gathered{p}") for p in range(PASSES)]
        far_used = sem("far_used")
        far_moved = sem("far_moved")
        far_deg = sem("far_deg_step")
        far_dsum = sem("far_deg_used")
        USES = [ITERS + 1] + [ITERS] * (U - 1)

        def each_group(eng, body):
            with eng.Fori(0, ITERS) as it:
                for u in range(U):
                    body(it * U + u, it, u, P)
            body(FULL, ITERS, 0, TP)

        def if_far(eng, sweep):
            any_far = eng.value_load(flag_i[0:1, 0:1], min_val=0, max_val=1)
            with eng.If(any_far > 0):
                sweep()

        def each_slow(eng, body):
            with eng.Fori(0, FULL) as s:
                body(s, P)
            body(FULL, TP)

        def windows(eng, kind, first, k, of):
            return nc.values_load_multi_w_load_instructions(
                of[0:1, bass.ds(first, k)], engines=[kind], min_val=0,
                max_val=NA - 1 if of is win_row else (NB - 1) * BK + NB * (BA - 1),
                skip_runtime_bounds_check_because="a window starts at the least of its group's targets, which are nodes")[1]

        def by_group(t, s):
            return t[:, bass.ds(s, 1), :].rearrange("p s k -> p (s k)")

        block = ctx.enter_context(nc.Block())

        @block.sync
        def _(sp):
            def load_rows(tile, dram, s):
                q = CH - 1
                n = q * P * GE
                end = FULL * GE
                sp.dma_start(tile[:, 0:q, :], dram[0:n].rearrange("(c q e) -> q c e", q=P, e=GE)).then_inc(s, 16)
                sp.dma_start(tile[0:LASTQ - 1, q, :], dram[n:end].rearrange("(q e) -> q e", e=GE)).then_inc(s, 16)
                sp.dma_start(tile[LASTQ - 1:LASTQ, q, 0:G * TP],
                             dram[end:E].rearrange("(a e) -> a e", a=1)).then_inc(s, 16)
                sp.dma_start(tile[LASTQ - 1:LASTQ, q, G * TP:GE],
                             dram[E - (GE - G * TP):E].rearrange("(a e) -> a e", a=1)).then_inc(s, 16)

            def node_dma(to_dram, dram, tile, c0, c1, s):
                d = dram.rearrange("(p j) f -> p j f", j=J)
                for a, b in ((0, PK), (PK, PN)):
                    there, here = d[a:b, c0:c1, :], tile[a:b, c0:c1, :]
                    sp.dma_start(*((there, here) if to_dram else (here, there))).then_inc(s, 16)

            load_rows(dst_i, dst, s_dst)
            load_rows(src_i, src, s_src)
            load_rows(row_wgt, edge_weight, s_wgt)
            node_dma(False, x, x_sb, 0, J, s_x)
            for t, w in ((w_c[:, 0, :], c1_w), (w_c[:, 1, :], c2_w), (w_g[:, 0, :], g1_w), (w_g[:, 1, :], g2_w)):
                sp.dma_start(t, w).then_inc(s_par, 16)
            for k, b in enumerate((c1_b, c2_b, be)):
                sp.dma_start(bias_b[:, k, :], b.rearrange("(a n) -> a n", a=1).to_broadcast([PN, F])).then_inc(s_par, 16)
            for k, b in enumerate((g1_b, g2_b, gamma, beta)):
                sp.dma_start(colv[:, k:k + 1], b.rearrange("(n a) -> n a", a=1)).then_inc(s_par, 16)
            sp.wait_ge(s_blk0, 1)
            for g in range(G):
                sp.dma_start(we_blk[KE * g:KE * g + KE, F * g:F * g + F], we).then_inc(s_blk, 16)

            sp.wait_ge(s_dc, CA)
            for c in range(CA):
                n = min(P, NA - c * P)
                sp.dma_start(deg_lin[c * P * AL:(c * P + n) * AL].rearrange("(q b) -> q b", b=AL),
                             degT[0:n, c, :]).then_inc(s_dout, 16)
            sp.wait_ge(s_dout, 16 * CA)
            sp.dma_start(deg[:, :], deg_lin[0:N].rearrange("(p j) -> p j", j=J)).then_inc(s_din, 16)

            for p in range(PASSES):
                for c in range(NC):
                    if p == 1:
                        sp.wait_ge(s_relu, ((c + 1) * QC + 1) // 2 * JQ)
                        sp.wait_ge(s_relu_v, (c + 1) * QC // 2)
                    elif p == 0:
                        sp.wait_ge(s_tab, c + 1)
                    else:
                        sp.wait_ge(s_be, c + 1)
                    node_dma(True, table[p], tab, c * JC, (c + 1) * JC, s_tabw)

            def load_ea(ring, s, u, np_):
                sp.wait_ge(ring.tr, s + 1)
                sp.dma_start(ea[u][0:np_, :],
                             edge_attr[bass.ds(s * GE, G * np_), :].rearrange("(p g) k -> p (g k)", g=G)
                             ).then_inc(ring.ea[u], 16)

            each_group(sp, lambda s, it, u, np_: load_ea(fast, s, u, np_))

            def sweep():
                sp.wait_ge(fast.tr, NS + U)
                each_slow(sp, lambda s, np_: load_ea(slow, s, 0, np_))

            if_far(sp, sweep)

            for c in range(NC):
                sp.wait_ge(s_ya, (c + 1) * QC)
                node_dma(True, out, x_sb, c * JC, (c + 1) * JC, s_out)
            sp.wait_ge(s_out, 32 * NC)

        @block.gpsimd
        def _(pool):
            pool.memset(we_blk[:, :], 0.0).then_inc(s_blk0, 1)
            pool.iota(iota_i[:, :], pattern=[[1, SW]], base=0, channel_multiplier=0).then_inc(s_const, 1)
            pool.memset(ident[:, :], 0.0).then_inc(s_const, 1)
            pool.wait_ge(s_const, 2)
            pool.affine_select(out=ident[:, :], in_=ident[:, :], compare_op=ALU.not_equal, fill=1.0,
                               base=0, pattern=[[-1, P]], channel_multiplier=1).then_inc(s_const, 1)

            def gather(ring, p, s, u, np_, got):
                pool.wait_ge(ring.staged, p * NS + s + 1)
                pool.sem_inc(ring.issue, 1)
                for g in range(G):
                    pool.indirect_dma_start(
                        out=rows_g[u][0:np_, g * F:(g + 1) * F], out_offset=None, in_=table[p],
                        in_offset=bass.IndirectOffsetOnAxis(ap=idx[u][0:np_, g:g + 1], axis=0),
                    ).then_inc(got, 16)

            def centre(c):
                js = slice(c * JC, (c + 1) * JC)
                m = mean[:, js].unsqueeze(2).to_broadcast([PN, JC, F])
                pool.tensor_tensor(tab[:, js, :], x_sb[:, js, :], m, ALU.subtract).then_inc(s_cent, 1)

            def add_be(c):
                js = slice(c * JC, (c + 1) * JC)
                b = bias_b[:, 2, :].unsqueeze(1).to_broadcast([PN, JC, F])
                pool.wait_ge(s_nt, 2 * NQ + (c + 1) * QC)
                pool.tensor_tensor(tab[:, js, :], tab[:, js, :], b, ALU.add).then_inc(s_be, 1)

            pool.wait_ge(s_trc, 4 * CH)
            w4 = edge[:, :, 2 * G:3 * G]
            v4 = lambda t: t.rearrange("p (s g) -> p s g", g=G)
            left, n = w4, 0
            for k in range(NB):
                here = wgt3[:, :, k].rearrange("p (s g) -> p s g", g=G)
                pool.tensor_copy(here, left).then_inc(s_w3a if k == NB - 1 else s_w3, 1)
                if k < NB - 1:
                    pool.wait_ge(s_w3, n + 1)
                    pool.tensor_tensor(v4(wgt_r), left, here, ALU.subtract).then_inc(s_w3, 1)
                    left, n = v4(wgt_r), n + 2
                    pool.wait_ge(s_w3, n)

            pool.wait_ge(s_par, 16 * 11)
            pool.wait_ge(s_mean, 1)
            pool.wait_ge(s_tr, 4 * CH)
            for c in range(NC):
                centre(c)

            for p in range(PASSES):
                if p == 2:
                    for c in range(NC):
                        pool.wait_ge(s_mean, 1 + c + 1)
                        pool.wait_ge(s_expd, c + 1)
                        centre(c)
                        if c >= 1:
                            add_be(c - 1)
                    add_be(NC - 1)
                pool.wait_ge(s_tabw, 32 * NC * (p + 1))
                each_group(pool, lambda s, it, u, np_: gather(fast, p, s, u, np_, fast_got[u]))
                if_far(pool, lambda: each_slow(pool, lambda s, np_: gather(slow, p, s, 0, np_, slow_got[p])))

            pool.wait_ge(s_logz, 1)
            for c in range(NC):
                js = slice(c * JC, (c + 1) * JC)
                lz = logz[:, js].unsqueeze(2).to_broadcast([PN, JC, F])
                pool.tensor_tensor(x_sb[:, js, :], x_sb[:, js, :], lz, ALU.subtract).then_inc(s_x1, 1)

        @block.scalar
        def _(act):
            act.sem_inc(fast.trc, U)
            act.sem_inc(slow.trc, 1)

            for n in range(4 * CH):
                c, k = divmod(n, 4)
                nq = P if c < CH - 1 else LASTQ
                act.wait_ge(s_tr, n + 1)
                act.activation(edge[:, c * P:c * P + nq, k * G:(k + 1) * G],
                               bank[n % 2][:, 0:G * nq].rearrange("p (g q) -> p q g", g=G),
                               ACT.Copy).then_inc(s_trc, 1)

            def root(n, o, i):
                act.wait_ge(s_root, n + 1)
                act.activation(o, i, ACT.Sqrt).then_inc(s_rooted, 1)

            def copy_nodes(p, q):
                act.wait_ge(s_nt, p * NQ + q + 1)
                act.activation(acc_j[:, q * JQ:(q + 1) * JQ, :],
                               bank[3 + q % 2][0:F, 0:JQ * PN].rearrange("f (j p) -> f j p", j=JQ),
                               ACT.Copy).then_inc(s_ntc, 1)

            def stage(ring, p, s, u, np_):
                e = by_group(edge[0:np_, :, :], s)
                act.activation(attr[u][0:np_, :], e[:, G:4 * G], ACT.Copy)
                act.activation(idx[u][0:np_, :], e[:, 0:G], ACT.Copy).then_inc(ring.staged, 1)

            def stage_fast(p, s, u, np_):
                act.wait_ge(fast.agg, p * NS + s + 1)
                stage(fast, p, s, u, np_)

            def stage_slow(p, s, np_):
                act.wait_ge(slow.added, (p * NS + s) * NW + 1)
                stage(slow, p, s, 0, np_)

            def copy_eaT(ring, s, k, np_):
                act.wait_ge(ring.tr, s + k + ring.slots)
                act.wait_ge(ring.lin, s + ring.slots)
                w = (k - 1) * P + np_
                act.activation(eaT[:, 0:w], ps_t[:, 0:w], ACT.Copy).then_inc(ring.trc, k)

            def relu_msg(ring, s, u, np_):
                act.wait_ge(ring.msg, s + 1 + ring.slots)
                act.activation(rows_g[u][0:np_, :], rows_g[u][0:np_, :], ACT.Relu).then_inc(ring.relu, 1)

            def sweep(p):
                def one(s, np_):
                    stage_slow(p, s, np_)
                    if p == 2:
                        copy_eaT(slow, s, 1, np_)
                        relu_msg(slow, s, 0, np_)
                act.wait_ge(fast.agg, U + (p + 1) * NS)
                each_slow(act, one)

            root(0, root_out[:, :], root_in[:, :])
            root(1, root_out[:, :], root_in[:, :])
            act.wait_ge(s_flag, 1)
            for q in range(NQ):
                copy_nodes(0, q)
            each_group(act, lambda s, it, u, np_: stage_fast(0, s, u, np_))
            if_far(act, lambda: sweep(0))

            LAG = 3
            for q in range(NQ + LAG):
                if q < NQ and q % 2 == 0:
                    for j in range(q * JQ, (q + 1) * JQ):
                        act.wait_ge(s_linv, j + 1)
                        act.activation(tab[:, j, :], tab[:, j, :], ACT.Relu, scale=dinv[:, j:j + 1]).then_inc(s_relu, 1)
                if q >= LAG:
                    copy_nodes(1, q - LAG)
            act.wait_ge(fast.agg, U + NS)
            each_group(act, lambda s, it, u, np_: stage_fast(1, s, u, np_))
            if_far(act, lambda: sweep(1))

            for c in range(NC):
                act.wait_ge(s_exp, c + 1)
                for j in range(c * JC, (c + 1) * JC):
                    last = act.activation(tab[:, j, :], tab[:, j, :], ACT.Exp, bias=nmax[:, j:j + 1],
                                          accum_out=esum[:, j:j + 1])
                last.then_inc(s_expd, 1)
                cc = slice(c * JC, (c + 1) * JC)
                root(2 + c, root_out[:, cc], root_in[:, cc])
                if c >= 2:
                    for q in range((c - 2) * QC, (c - 1) * QC):
                        copy_nodes(2, q)
            for q in range((NC - 2) * QC, NQ):
                copy_nodes(2, q)
            act.wait_ge(s_expd, NC)
            act.activation(esum[:, :], esum[:, :], ACT.Ln).then_inc(s_ln, 1)

            act.wait_ge(fast.agg, U + 2 * NS)
            for u in range(U):
                stage_fast(2, u, u, P)

            def gin_body(s0, last):
                copy_eaT(fast, s0, U, P)
                for u in range(U):
                    relu_msg(fast, s0 + u, u, P)
                    if not last:
                        stage_fast(2, s0 + U + u, u, P)
                    elif u == 0:
                        stage_fast(2, FULL, 0, TP)

            with act.Fori(0, ITERS - 1) as it:
                gin_body(it * U, False)
            gin_body(FULL - U, True)
            copy_eaT(fast, FULL, 1, TP)
            relu_msg(fast, FULL, 0, TP)
            if_far(act, lambda: sweep(2))

            for w in range(NW):
                act.wait_ge(s_m1, w + 1)
                act.activation(z1[w % 2], bank[w % 2][0:F, 0:SW], ACT.Relu, bias=colv[:, 0:1]).then_inc(s_z1, 1)
                if w >= 1:
                    act.wait_ge(s_m2, w)
                    act.activation(acc[:, (w - 1) * SW:w * SW], bank[2 + (w - 1) % 2][0:F, 0:SW], ACT.Identity,
                                   bias=colv[:, 1:2]).then_inc(s_z2, 1)
            act.wait_ge(s_m2, NW)
            act.activation(acc[:, (NW - 1) * SW:N], bank[2 + (NW - 1) % 2][0:F, 0:SW], ACT.Identity,
                           bias=colv[:, 1:2]).then_inc(s_z2, 1)
            root(2 + NC, bnv[:, 3:4], bnv[:, 2:3])
            act.wait_ge(s_bn, 1)
            act.activation(acc[:, 0:N], acc[:, 0:N], ACT.Relu, scale=bnv[:, 6:7], bias=bnv[:, 7:8]).then_inc(s_y, 1)

        @block.tensor
        def _(pe):
            for r, n in ((fast, U), (slow, 1)):
                pe.sem_inc(r.agg, n)
                pe.sem_inc(r.tr, n)
                pe.sem_inc(r.lin, n)
            pe.sem_inc(far_used, 1)
            pe.sem_inc(far_dsum, 1)
            pe.sem_inc(s_dsum, 2)

            pe.wait_ge(s_const, 3)
            pe.wait_ge(s_rows, 1)
            pe.wait_ge(s_wgt, 64)
            for n in range(4 * CH):
                c, k = divmod(n, 4)
                nq = P if c < CH - 1 else LASTQ
                if n >= 2:
                    pe.wait_ge(s_trc, n - 1)
                for g in range(G):
                    last = pe.transpose(bank[n % 2][:, g * nq:(g + 1) * nq], row[k][0:nq, c, g:GE:G], ident[0:nq, 0:nq])
                last.then_inc(s_tr, 1)
            for c in range(CH):
                pe.transpose(bank[2][0:1, c * P:(c + 1) * P], win_f[:, c:c + 1], ident[:, :])
                last = pe.transpose(bank[3][0:1, c * P:(c + 1) * P], span_f[:, c:c + 1], ident[:, :])
            last.then_inc(s_wt, 1)

            def zero_deg(first):
                pe.matmul(ps_degf, zeros[:, 0:2 * AL].bitcast(F32), zeros[:, 0:2 * NA].bitcast(F32), start=first, stop=not first)
                for k in range(NB):
                    last = pe.matmul(ps_deg[:, k * BK:k * BK + NB * (BA + WA)], zeros[:, 0:AL],
                                     zeros[:, 0:NB * (BA + WA)], start=first, stop=not first)
                return last

            pe.wait_ge(s_zero, 1)
            zero_deg(True)
            pe.wait_ge(s_flag, 1)

            def deg_step(n, w, k, np_):
                pe.wait_ge(s_dhot, n + 1)
                for i in range(len(w)):
                    for g in range(G):
                        t = i * G + g
                        last = pe.matmul(ps_deg[:, bass.ds(w[i], WA * NB)], hot_b[k][0:np_, t, :],
                                         hot_w[k][0:np_, t, :, :].rearrange("p a k -> p (a k)"), start=False, stop=False)
                last.then_inc(s_dsum, 1)

            with pe.Fori(0, FULL // (2 * DG)) as it:
                w = windows(pe, mybir.EngineType.PE, it * 2 * DG, 2 * DG, bank_row)
                for k in range(2):
                    deg_step(it * 2 + k, w[k * DG:(k + 1) * DG], k, P)
            deg_step(FULL // DG, windows(pe, mybir.EngineType.PE, FULL, 1, bank_row), 0, TP)

            def deg_sweep():
                def one(s, np_):
                    pe.wait_ge(far_deg, 6 * s + 6)
                    for g in range(G):
                        last = pe.matmul(ps_degf, hot[0][0:np_, g, 0:AL], far[0:np_, g, 0:NA],
                                         start=False, stop=False)
                    last.then_inc(far_dsum, 1)
                each_slow(pe, one)

            if_far(pe, deg_sweep)
            zero_deg(False).then_inc(s_dall, 1)
            pe.wait_ge(s_dsb, 1)
            for c in range(CA):
                n = min(P, NA - c * P)
                last = pe.transpose(bank[2][0:n, c * AL:(c + 1) * AL], deg_sb[:, c * P:c * P + n], ident[0:AL, 0:AL])
            last.then_inc(s_dT, 1)

            def transpose_nodes(p, q):
                if q >= 2:
                    pe.wait_ge(s_ntc, p * NQ + q - 1)
                for i in range(JQ):
                    last = pe.transpose(bank[3 + q % 2][0:F, i * PN:(i + 1) * PN], tab[:, q * JQ + i, :], ident[0:PN, 0:PN])
                last.then_inc(s_nt, 1)

            def transpose_ea(ring, s, first, it, u, np_):
                pe.wait_ge(ring.ea[u], 16 * (it + 1))
                pe.wait_ge(ring.trc, first + ring.slots)
                pe.transpose(ps_t[:, u * P:u * P + np_], ea[u][0:np_, :], ident[0:np_, 0:np_]).then_inc(ring.tr, 1)

            def linear_ea(ring, s, upto, u, np_):
                pe.wait_ge(ring.trc, upto + ring.slots)
                pe.wait_ge(ring.msg, s + 1)
                pe.matmul(ps_e[u][0:np_, :], eaT[:, u * P:u * P + np_], we_blk[:, :], start=True, stop=True).then_inc(ring.lin, 1)

            def aggregate(p, s, it, u, np_):
                n = p * NS + s
                pe.wait_ge(fast.hot, n + 1)
                pe.wait_ge(fast.added, n + 1)
                if p < 2:
                    pe.wait_ge(fast_got[u], 16 * G * (p * USES[u] + it + 1))
                else:
                    pe.wait_ge(fast.relu, s + 1)
                for g in range(G):
                    last = pe.matmul(ps_agg[u], rows_g[u][0:np_, g * F:(g + 1) * F], hot[u][0:np_, g, :],
                                     start=g == 0, stop=g == G - 1)
                last.then_inc(fast.agg, 1)

            def sweep(p):
                def one(s, np_):
                    n = p * NS + s
                    if p == 2:
                        transpose_ea(slow, s, s, s, 0, np_)
                        linear_ea(slow, s, s + 1, 0, np_)
                    with pe.Fori(0, NW) as w:
                        if p == 2:
                            pe.wait_ge(slow.relu, s + 1)
                        else:
                            pe.wait_ge(slow_got[p], 16 * G * (s + 1))
                        pe.wait_ge(slow.hot, n * NW + w + 1)
                        pe.wait_ge(slow.added, n * NW + w + 1)
                        for g in range(G):
                            last = pe.matmul(ps_far, rows_g[0][0:np_, g * F:(g + 1) * F], far[0:np_, g, :],
                                             start=g == 0, stop=g == G - 1)
                        last.then_inc(far_used, 1)
                each_slow(pe, one)
                pe.wait_ge(slow.added, (p + 1) * NS * NW + 1)

            def linear(p, q):
                if q >= 3:
                    pe.wait_ge(s_linv, p * J + (q - 2) * JQ)
                for i in range(JQ):
                    last = pe.matmul(bank[q % 3][0:PN, i * F:(i + 1) * F], acc_j[:, q * JQ + i, :], w_c[:, p, :],
                                     start=True, stop=True)
                last.then_inc(s_lin, 1)

            for c in range(NC):
                pe.wait_ge(s_tab, c + 1)
                for q in range(c * QC, (c + 1) * QC):
                    transpose_nodes(0, q)
            each_group(pe, lambda s, it, u, np_: aggregate(0, s, it, u, np_))
            pe.wait_ge(fast.added, U + NS)
            if_far(pe, lambda: sweep(0))

            pe.wait_ge(s_par, 16 * 11)
            LAG = 3
            for q in range(NQ + LAG):
                if q < NQ:
                    linear(0, q)
                if q >= LAG:
                    if (q - LAG) % 2 == 0:
                        pe.wait_ge(s_relu, ((q - LAG) // 2 + 1) * JQ)
                    else:
                        pe.wait_ge(s_relu_v, (q - LAG + 1) // 2)
                    transpose_nodes(1, q - LAG)
            each_group(pe, lambda s, it, u, np_: aggregate(1, s, it, u, np_))
            pe.wait_ge(fast.added, U + 2 * NS)
            if_far(pe, lambda: sweep(1))

            for c in range(NC + 2):
                if c < NC:
                    for q in range(c * QC, (c + 1) * QC):
                        linear(1, q)
                if c >= 2:
                    pe.wait_ge(s_tab, NC + c - 1)
                    for q in range((c - 2) * QC, (c - 1) * QC):
                        transpose_nodes(2, q)

            pe.wait_ge(s_blk, 16 * G)
            def gin_body(s0, it):
                for u in range(U):
                    transpose_ea(fast, s0 + u, s0, it, u, P)
                for u in range(U):
                    linear_ea(fast, s0 + u, s0 + U, u, P)
                for u in range(U):
                    aggregate(2, s0 + u, it, u, P)
            with pe.Fori(0, ITERS) as it:
                gin_body(it * U, it)
            transpose_ea(fast, FULL, FULL, ITERS, 0, TP)
            linear_ea(fast, FULL, NS, 0, TP)
            aggregate(2, FULL, ITERS, 0, TP)
            pe.wait_ge(fast.added, U + 3 * NS)
            if_far(pe, lambda: sweep(2))

            for w in range(NW + 1):
                if w < NW:
                    if w >= 2:
                        pe.wait_ge(s_z1, w - 1)
                    pe.matmul(bank[w % 2][0:F, 0:SW], w_g[:, 0, :], acc[:, w * SW:(w + 1) * SW],
                              start=True, stop=True).then_inc(s_m1, 1)
                if w >= 1:
                    v = w - 1
                    pe.wait_ge(s_z1, w)
                    if v >= 2:
                        pe.wait_ge(s_z2, v - 1)
                    pe.matmul(bank[2 + v % 2][0:F, 0:SW], w_g[:, 1, :], z1[v % 2],
                              start=True, stop=True).then_inc(s_m2, 1)
            pe.wait_ge(s_y, 1)
            for q in range(NQ):
                if q >= 3:
                    pe.wait_ge(s_ya, q - 2)
                for i in range(JQ):
                    last = pe.transpose(bank[4 + q % 3][0:PN, i * F:(i + 1) * F], acc_j[:, q * JQ + i, :], ident[0:F, 0:F])
                last.then_inc(s_yt, 1)

        @block.vector
        def _(dve):
            for r, n in ((fast, U), (slow, 1)):
                dve.sem_inc(r.added, n)
                dve.sem_inc(r.msg, n)

            steps = [0]

            def then(ins):
                steps[0] += 1
                ins.then_inc(s_v, 1)
                dve.wait_ge(s_v, steps[0])

            def parts(f):
                f(slice(0, P), slice(0, CH - 1))
                return f(slice(0, LASTQ), slice(CH - 1, CH))

            dve.memset(acc_t[:, N:], 0.0)
            dve.memset(win_f[:, :], 0.0)
            then(dve.memset(span_f[:, :], 0.0))
            dve.memset(zeros[:, :], 0.0).then_inc(s_zero, 1)
            dve.wait_ge(s_const, 3)
            dve.tensor_copy(iota[:, :], iota_i[:, :])

            dve.wait_ge(s_dst, 64)
            then(parts(lambda q, c: dve.tensor_copy(row_dst[q, c, :], dst_i[q, c, :])))
            parts(lambda q, c: dve.tensor_reduce(least[q, c], row_dst[q, c, :], AX.X, ALU.min))
            then(parts(lambda q, c: dve.tensor_reduce(most[q, c], row_dst[q, c, :], AX.X, ALU.max)))
            then(parts(lambda q, c: dve.tensor_copy(base_i[q, c], least[q, c])))
            then(parts(lambda q, c: dve.tensor_single_scalar(win_i[q, c], base_i[q, c], 5, ALU.arith_shift_right)))
            then(parts(lambda q, c: dve.tensor_copy(win_f[q, c], win_i[q, c])))
            then(parts(lambda q, c: dve.tensor_scalar(base_f[q, c], win_f[q, c], float(AL), None, ALU.mult)))
            parts(lambda q, c: dve.tensor_tensor(span_f[q, c], most[q, c], base_f[q, c], ALU.subtract))
            for c in range(CH):
                q = slice(0, P if c < CH - 1 else LASTQ)
                last = dve.tensor_scalar(row_rel[q, c, :], row_dst[q, c, :], base_f[q, c:c + 1], None, ALU.subtract)
            then(last)
            then(parts(lambda q, c: dve.tensor_scalar(row_far[q, c, :], row_rel[q, c, :], float(W), FAR, ALU.is_lt, ALU.mult)))
            parts(lambda q, c: dve.tensor_tensor(row_far[q, c, :], row_far[q, c, :], row_dst[q, c, :], ALU.add))
            dve.wait_ge(s_src, 64)
            parts(lambda q, c: dve.tensor_copy(row_src[q, c, :], src_i[q, c, :])).then_inc(s_rows, 1)

            def ln_stats(c):
                for j in range(c * JC, (c + 1) * JC):
                    last = dve.bn_stats(stat[:, j, :], x_sb[:, j, :])
                return last

            def ln_rstd_start(js):
                me, mo, ve, vo = (stat[:, js, k] for k in (1, 4, 2, 5))
                m, r, t = mean[:, js], root_in[:, js], tmp_j[:, js]
                dve.tensor_tensor(m, me, mo, ALU.add)
                dve.tensor_tensor(t, me, mo, ALU.subtract)
                then(dve.tensor_tensor(r, ve, vo, ALU.add))
                dve.tensor_scalar(m, m, 0.5, None, ALU.mult).then_inc(s_mean, 1)
                then(dve.tensor_tensor(t, t, t, ALU.mult))
                then(dve.tensor_scalar(r, r, 1.0 / F, EPS, ALU.mult, ALU.add))
                dve.scalar_tensor_tensor(r, t, 0.25, r, ALU.mult, ALU.add).then_inc(s_root, 1)

            dve.wait_ge(s_x, 32)
            for c in range(NC):
                last = ln_stats(c)
            then(last)
            ln_rstd_start(slice(0, J))

            dve.wait_ge(s_wt, 1)
            dve.tensor_copy(win_row[0:1, :], bank[2][0:1, 0:CH * P])
            for k in range(1, NB):
                dve.tensor_scalar(row_f[:, k, :], bank[2][0:1, 0:CH * P], float(k * BA), float(BK - NB * BA), ALU.is_ge, ALU.mult)
            then(dve.tensor_scalar(row_f[:, 0, :], bank[2][0:1, 0:CH * P], float(NB), None, ALU.mult))
            then(dve.tensor_tensor(row_f[:, 0, :], row_f[:, 0, :], row_f[:, 1, :], ALU.add))
            then(dve.tensor_tensor(bank_row[:, :], row_f[:, 0, :], row_f[:, 2, :], ALU.add))
            then(dve.tensor_reduce(flag_f[0:1, :], bank[3][0:1, 0:CH * P], AX.X, ALU.max))
            dve.tensor_scalar(flag_i[0:1, :], flag_f[0:1, :], float(W), None, ALU.is_ge).then_inc(s_flag, 1)

            dve.wait_ge(s_trc, 4 * CH)
            v3 = lambda t: t.rearrange("p (s g) -> p s g", g=G)
            then(dve.tensor_copy(v3(col_i), edge[:, :, G:2 * G]))
            then(dve.tensor_single_scalar(col_i2, col_i, AL - 1, ALU.bitwise_and))
            dve.tensor_copy(col_b, col_i2)
            then(dve.tensor_single_scalar(col_i, col_i, 5, ALU.arith_shift_right))
            then(dve.tensor_copy(col_a, col_i))

            def deg_hot(n, s0, k, ng, np_):
                t = ng * G
                cols = lambda a: a[0:np_, bass.ds(s0 * G, t)].unsqueeze(2)
                dve.wait_ge(s_dsum, n + 1)
                ib = iota[0:np_, 0:AL].unsqueeze(1).to_broadcast([np_, t, AL])
                ia = iota[0:np_, 0:WA].unsqueeze(1).to_broadcast([np_, t, WA])
                dve.tensor_tensor(hot_a[k][0:np_, 0:t, :], ia, cols(col_a).to_broadcast([np_, t, WA]), ALU.is_equal).then_inc(s_dha, 1)
                dve.tensor_tensor(hot_b[k][0:np_, 0:t, :], ib, cols(col_b).to_broadcast([np_, t, AL]), ALU.is_equal)
                a4 = hot_a[k][0:np_, 0:t, :].unsqueeze(3).to_broadcast([np_, t, WA, NB])
                w4 = wgt3[0:np_, bass.ds(s0 * G, t), :].unsqueeze(2).to_broadcast([np_, t, WA, NB])
                dve.wait_ge(s_dha, n + 1)
                dve.tensor_tensor(hot_w[k][0:np_, 0:t, :, :], a4, w4, ALU.mult).then_inc(s_dhot, 1)

            dve.wait_ge(s_w3a, 1)
            with dve.Fori(0, FULL // (2 * DG)) as it:
                for k in range(2):
                    deg_hot(it * 2 + k, it * 2 * DG + k * DG, k, DG, P)
            deg_hot(FULL // DG, FULL, 0, 1, TP)

            def deg_sweep():
                dve.wait_ge(s_dsum, FULL // DG + 3)
                def one(s, np_):
                    k = 6 * s
                    o = slice(0, np_)
                    dve.wait_ge(far_dsum, s + 1)
                    dve.tensor_copy(far_i[o, 0, :], by_group(edge[o, :, :], s)[:, 3 * G:4 * G]).then_inc(far_deg, 1)
                    dve.wait_ge(far_deg, k + 1)
                    dve.tensor_single_scalar(far_i[o, 1, :], far_i[o, 0, :], AL - 1, ALU.bitwise_and).then_inc(far_deg, 1)
                    dve.tensor_single_scalar(far_i[o, 2, :], far_i[o, 0, :], 5, ALU.arith_shift_right).then_inc(far_deg, 1)
                    dve.wait_ge(far_deg, k + 3)
                    dve.tensor_copy(far_c[o, :, :], far_i[o, 1:3, :]).then_inc(far_deg, 1)
                    dve.tensor_copy(attr[0][o, 0:G], by_group(edge[o, :, :], s)[:, 2 * G:3 * G]).then_inc(far_deg, 1)
                    dve.wait_ge(far_deg, k + 5)
                    for g in range(G):
                        dve.tensor_scalar(hot[0][o, g, 0:AL], iota[o, 0:AL], far_c[o, 0, g:g + 1], None, ALU.is_equal)
                        last = dve.tensor_scalar(far[o, g, 0:NA], iota[o, 0:NA], far_c[o, 1, g:g + 1],
                                                 attr[0][o, g:g + 1], ALU.is_equal, ALU.mult)
                    last.then_inc(far_deg, 1)
                each_slow(dve, one)

            if_far(dve, deg_sweep)
            dve.wait_ge(s_dall, 1)
            then(dve.memset(deg_sb, 0.0))
            dve.tensor_copy(deg_sb[:, 0:NA], ps_degf)
            for k in range(NB):
                last = dve.tensor_reduce(deg_k[:, k * (BA + WA):(k + 1) * (BA + WA)],
                                         ps_deg[:, k * BK:k * BK + NB * (BA + WA)].rearrange("b (a k) -> b a k", k=NB), AX.X, ALU.add)
            then(last)
            for k in range(NB):
                a = deg_sb[:, k * BA:(k + 1) * BA + WA]
                last = dve.tensor_tensor(a, a, deg_k[:, k * (BA + WA):(k + 1) * (BA + WA)], ALU.add)
                if k < NB - 1:
                    then(last)
            last.then_inc(s_dsb, 1)
            dve.wait_ge(s_dT, 1)
            for c in range(CA):
                n = min(P, NA - c * P)
                dve.tensor_copy(degT[0:n, c, :], bank[2][0:n, c * AL:(c + 1) * AL]).then_inc(s_dc, 1)
            dve.wait_ge(s_rooted, 1)
            then(dve.reciprocal(rstd[:, :], root_out[:, :]))
            dve.wait_ge(s_din, 16)
            then(dve.tensor_scalar(deg[:, :], deg[:, :], 1.0, None, ALU.add))
            dve.tensor_scalar(root_in[:, :], deg[:, :], TINY, None, ALU.max).then_inc(s_root, 1)
            dve.tensor_scalar(tmp_j[:, :], deg[:, :], 0.0, None, ALU.is_gt)
            dve.wait_ge(s_rooted, 2)
            then(dve.reciprocal(dinv[:, :], root_out[:, :]))
            then(dve.tensor_tensor(dinv[:, :], dinv[:, :], tmp_j[:, :], ALU.mult))
            then(dve.tensor_tensor(tmp_j[:, :], dinv[:, :], rstd[:, :], ALU.mult))

            def chunk(t, c):
                return t[:, c * JC:(c + 1) * JC, :]

            def bc(t, c):
                return t[:, c * JC:(c + 1) * JC].unsqueeze(2).to_broadcast([PN, JC, F])

            for c in range(NC):
                dve.wait_ge(s_cent, c + 1)
                dve.scalar_tensor_tensor(chunk(tab, c), chunk(tab, c), 0.0, bc(tmp_j, c), ALU.max, ALU.mult).then_inc(s_tab, 1)

            def build_hot(p, s, u, np_):
                dve.wait_ge(fast.staged, p * NS + s + 1)
                for g in range(G):
                    rel = attr[u][0:np_, g:g + 1]
                    if p < 2:
                        last = dve.tensor_scalar(hot[u][0:np_, g, :], iota[0:np_, 0:W], rel,
                                                 attr[u][0:np_, G + g:G + g + 1], ALU.is_equal, ALU.mult)
                    else:
                        last = dve.tensor_scalar(hot[u][0:np_, g, :], iota[0:np_, 0:W], rel, None, ALU.is_equal)
                last.then_inc(fast.hot, 1)

            def add_window(p, s, u, w0):
                n = p * NS + s
                dve.wait_ge(fast.agg, n + 1 + U)
                dve.wait_ge(fast.added, n + U)
                a = acc[:, bass.ds(w0 * AL, W)]
                dve.tensor_tensor(a, a, ps_agg[u], ALU.add).then_inc(fast.added, 1)

            def add_edge_term(ring, s, it, u, np_):
                dve.wait_ge(ring.lin, s + 1 + ring.slots)
                if ring is fast:
                    dve.wait_ge(fast_got[u], 16 * G * (2 * USES[u] + it + 1))
                else:
                    dve.wait_ge(slow_got[2], 16 * G * (s + 1))
                r = rows_g[u][0:np_, :]
                dve.tensor_tensor(r, r, ps_e[u][0:np_, :], ALU.add).then_inc(ring.msg, 1)

            def fast_pass(p):
                def body(it, us, np_, w):
                    s0 = it * U if us > 1 else FULL
                    for u in range(us):
                        build_hot(p, s0 + u, u, np_)
                    for u in range(us):
                        if p == 2:
                            add_edge_term(fast, s0 + u, it, u, np_)
                            if u >= 1:
                                add_window(p, s0 + u - 1, u - 1, w[u - 1])
                        else:
                            add_window(p, s0 + u, u, w[u])
                    if p == 2:
                        add_window(p, s0 + us - 1, us - 1, w[us - 1])
                dve.wait_ge(s_ntc, (p + 1) * NQ)
                with dve.Fori(0, ITERS) as it:
                    body(it, U, P, windows(dve, mybir.EngineType.DVE, it * U, U, win_row))
                body(ITERS, 1, TP, windows(dve, mybir.EngineType.DVE, FULL, 1, win_row))

            def sweep(p):
                def one(s, np_):
                    n = p * NS + s
                    o = slice(0, np_)
                    if p == 2:
                        add_edge_term(slow, s, s, 0, np_)
                    with dve.Fori(0, NW) as w:
                        m = n * NW + w
                        dve.wait_ge(slow.staged, n + 1)
                        dve.wait_ge(far_used, m + 1)
                        dve.wait_ge(far_moved, m + 1)
                        for g in range(G):
                            tgt = attr[0][o, 2 * G + g:2 * G + g + 1]
                            if p < 2:
                                last = dve.tensor_scalar(far[o, g, :], iota[o, :], tgt, attr[0][o, G + g:G + g + 1],
                                                         ALU.is_equal, ALU.mult)
                            else:
                                last = dve.tensor_scalar(far[o, g, :], iota[o, :], tgt, None, ALU.is_equal)
                        last.then_inc(slow.hot, 1)
                        dve.wait_ge(slow.hot, m + 1)
                        t = attr[0][o, 2 * G:3 * G]
                        dve.tensor_scalar(t, t, -float(SW), None, ALU.add).then_inc(far_moved, 1)
                        dve.wait_ge(far_used, m + 2)
                        dve.wait_ge(slow.added, m + 1)
                        a = acc[:, bass.ds(w * SW, SW)]
                        dve.tensor_tensor(a, a, ps_far, ALU.add).then_inc(slow.added, 1)
                dve.wait_ge(fast.added, U + (p + 1) * NS)
                if p == 0:
                    dve.sem_inc(far_moved, 1)
                each_slow(dve, one)

            def linear_read(p, q):
                dve.wait_ge(s_lin, p * NQ + q + 1)
                for i in range(JQ):
                    j = q * JQ + i
                    last = dve.scalar_tensor_tensor(tab[:, j, :], bank[q % 3][0:PN, i * F:(i + 1) * F], dinv[:, j:j + 1],
                                                    bias_b[:, p, :], ALU.mult, ALU.add).then_inc(s_linv, 1)

            fast_pass(0)
            if_far(dve, lambda: sweep(0))
            dve.wait_ge(s_par, 16 * 11)
            dve.wait_ge(s_tabw, 32 * NC)
            for q in range(NQ):
                linear_read(0, q)
                if q % 2:
                    t = tab[:, q * JQ:(q + 1) * JQ, :]
                    dve.wait_ge(s_linv, (q + 1) * JQ)
                    dve.scalar_tensor_tensor(t, t, 0.0, dinv[:, q * JQ:(q + 1) * JQ].unsqueeze(2).to_broadcast([PN, JQ, F]),
                                             ALU.max, ALU.mult).then_inc(s_relu_v, 1)
            fast_pass(1)
            if_far(dve, lambda: sweep(1))

            dve.wait_ge(s_tabw, 2 * 32 * NC)
            def finish(c):
                js = slice(c * JC, (c + 1) * JC)
                dve.wait_ge(s_rooted, 3 + c)
                then(dve.reciprocal(rstd[:, js], root_out[:, js]))
                dve.wait_ge(s_cent, NC + c + 1)
                dve.scalar_tensor_tensor(chunk(tab, c), chunk(tab, c), 0.0, bc(rstd, c), ALU.max, ALU.mult).then_inc(s_tab, 1)
            for c in range(NC):
                js = slice(c * JC, (c + 1) * JC)
                for q in range(c * QC, (c + 1) * QC):
                    linear_read(1, q)
                dve.wait_ge(s_linv, J + (c + 1) * JC)
                dve.tensor_tensor(chunk(x_sb, c), chunk(x_sb, c), chunk(tab, c), ALU.add)
                dve.tensor_reduce(nmax[:, js], chunk(tab, c), AX.X, ALU.max, negate=True).then_inc(s_exp, 1)
                dve.wait_ge(s_exp, c + 1)
                then(ln_stats(c))
                ln_rstd_start(js)
                if c >= 1:
                    finish(c - 1)
            finish(NC - 1)
            fast_pass(2)
            if_far(dve, lambda: sweep(2))

            dve.wait_ge(s_ln, 1)
            dve.tensor_tensor(logz[:, :], esum[:, :], nmax[:, :], ALU.subtract).then_inc(s_logz, 1)
            for w in range(NW):
                dve.wait_ge(s_z2, w + 1)
                last = dve.bn_stats(bn[:, w, :], acc[:, w * SW:(w + 1) * SW])
            then(last)
            then(dve.bn_aggr(bnv[:, 0:2], bn[:, :, :].rearrange("f w k -> f (w k)")))
            dve.tensor_scalar(bnv[:, 2:3], bnv[:, 1:2], EPS, None, ALU.add).then_inc(s_root, 1)
            dve.wait_ge(s_rooted, 3 + NC)
            then(dve.reciprocal(bnv[:, 4:5], bnv[:, 3:4]))
            then(dve.tensor_tensor(bnv[:, 6:7], bnv[:, 4:5], colv[:, 2:3], ALU.mult))
            then(dve.tensor_tensor(bnv[:, 5:6], bnv[:, 0:1], bnv[:, 6:7], ALU.mult))
            dve.tensor_tensor(bnv[:, 7:8], colv[:, 3:4], bnv[:, 5:6], ALU.subtract).then_inc(s_bn, 1)
            for q in range(NQ):
                dve.wait_ge(s_yt, q + 1)
                dve.wait_ge(s_x1, q // QC + 1)
                xs = x_sb[:, q * JQ:(q + 1) * JQ, :]
                dve.tensor_tensor(xs, xs, bank[4 + q % 3][0:PN, 0:JQ * F].rearrange("p (j f) -> p j f", j=JQ),
                                  ALU.add).then_inc(s_ya, 1)


_INS = ['x', 'src', 'dst', 'edge_attr_32', 'edge_weight', 'L0_gnn_W1', 'L0_gnn_b1', 'L0_gnn_W2', 'L0_gnn_b2',
        'L1_gnn_We', 'L1_gnn_be', 'L1_gnn_W1', 'L1_gnn_b1', 'L1_gnn_W2', 'L1_gnn_b2', 'L1_gnn_gamma', 'L1_gnn_beta']


def kernel(**inputs):
    import numpy as _np
    import concourse.bacc as _bacc
    from concourse import mybir as _mybir
    from concourse.bass_utils import run_bass_kernel_spmd as _run

    nc = _bacc.Bacc("TRN2", target_bir_lowering=False, num_devices=1)
    arrays, args = {}, []
    for name in _INS:
        a = _np.ascontiguousarray(inputs[name])
        arrays[f"in_{name}_dram"] = a
        args.append(nc.dram_tensor(f"in_{name}_dram", a.shape, _mybir.dt.from_np(a.dtype), kind="ExternalInput").ap())
    out = nc.dram_tensor("out_0_dram", inputs["x"].shape, _mybir.dt.float32, kind="ExternalOutput").ap()
    build_gnn(nc, *args, out)
    r = _run(nc, [arrays], core_ids=[0])
    return r.results[0]["out_0_dram"]
```

```python
import concourse.bass as bass
from concourse import mybir
from contextlib import ExitStack

F32 = mybir.dt.float32
I32 = mybir.dt.int32
BF16 = mybir.dt.bfloat16
ALU = mybir.AluOpType
ACT = mybir.ActivationFunctionType
AX = mybir.AxisListType


def build_gnn(nc, x, src, dst, edge_attr, edge_weight, c1_w, c1_b, c2_w, c2_b,
              we, be, g1_w, g1_b, g2_w, g2_b, gamma, beta, out):
    N, F = x.shape
    E = src.shape[0]
    KE = edge_attr.shape[1]
    P = 128
    G = 4
    GE = G * P
    NS = -(-E // GE)
    FULL = E // GE
    TP = (E - FULL * GE) // G
    U = 3
    ITERS = FULL // U
    DG = 10
    DK = 3
    CH = -(-NS // P)
    LASTQ = NS - (CH - 1) * P
    W = 128
    WARM = 10
    AL = 32
    WA = W // AL
    NA = -(-N // AL)
    BK = 512
    NB = 3
    BA = -(-NA // NB)
    CA = -(-NA // P)
    J = 100
    PN = N // J
    PK = PN // 16 * 16
    JC = 20
    NC = J // JC
    JQ = 4
    NQ = J // JQ
    QC = JC // JQ
    CUTS = (0, 3, 8, 13, 18, 22, 25)
    GC = len(CUTS) - 1
    SW = 500
    NW = N // SW
    FAR = -float(1 << 20)
    EPS = 1e-5
    TINY = 1.2e-38
    PASSES = 3
    assert FULL == NS - 1 and FULL % U == 0 and FULL % (DK * DG) == 0 and TP * G == E - FULL * GE and TP % 16 == 0
    assert N % J == 0 and N % SW == 0 and J % JC == 0 and JC % JQ == 0 and NA <= BK and NB * (BA + WA) <= BK

    table = [nc.dram_tensor(f"table{p}", (N, F), F32).ap() for p in range(PASSES)]
    deg_lin = nc.dram_tensor("deg_lin", (NA * AL,), F32).ap()

    ctx = ExitStack()
    with ctx:
        def sb(name, shape, dt=F32):
            return ctx.enter_context(nc.sbuf_tensor(name, shape, dt))

        def sem(name):
            return ctx.enter_context(nc.semaphore(name))

        x_sb = sb("x_sb", [PN, J, F])
        x_more_t = sb("x_more", [P, 2 * JC * F])
        x_more = x_more_t[0:PN, :].rearrange("p (k j f) -> p k j f", k=2, j=JC)
        tab_t = sb("tab", [P, J * F])
        tab = tab_t[0:PN, :].rearrange("p (j f) -> p j f", j=J)
        acc_t = sb("acc", [P, N + W])
        acc = acc_t[0:F, :]
        acc_j = acc[:, 0:N].rearrange("f (p j) -> f j p", j=J)
        edge = sb("edge", [P, NS, 4 * G])
        part = lambda t, k, n: t[:, k * n:(k + 1) * n]
        row = [part(tab_t, k, CH * GE).rearrange("q (c e) -> q c e", c=CH) for k in range(4)]
        row_src, row_rel, row_wgt, row_far = row
        dst_i = part(acc_t, 0, CH * GE).bitcast(I32).rearrange("q (c e) -> q c e", c=CH)
        src_i = part(acc_t, 1, CH * GE).bitcast(I32).rearrange("q (c e) -> q c e", c=CH)
        row_dst = part(acc_t, 2, CH * GE).rearrange("q (c e) -> q c e", c=CH)
        off = 3 * CH * GE
        col_b = part(acc_t[:, off:], 0, NS * G // 2).bitcast(BF16)
        col_a = part(acc_t[:, off:], 1, NS * G // 2).bitcast(BF16)
        col_i = part(acc_t, 1, NS * G).bitcast(I32)
        col_i2 = part(acc_t, 2, NS * G).bitcast(I32)
        deg_sb = part(acc_t, 2, NS * G)[0:AL, 0:NB * BA + WA]
        deg_k = part(acc_t, 1, NS * G)[0:AL, 0:NB * (BA + WA)]
        off2 = off + NS * G
        off3 = off2 + NB * NS * G // 2
        wgt3 = acc_t[:, off2:off3].bitcast(BF16).rearrange("p (k t) -> p k t", k=NB)
        iota_i = acc_t[:, off3:off3 + SW].bitcast(I32)
        iota_b = acc_t[:, off3 + SW:off3 + SW + AL * DG * G // 2].bitcast(BF16).rearrange("p (a t) -> p a t", t=DG * G)
        wgt_r = acc_t[:, 0:NS * G]
        least = sb("least", [P, CH])
        most = sb("most", [P, CH])
        win_i = sb("win_i", [P, CH], I32)
        base_i = sb("base_i", [P, CH], I32)
        win_f = sb("win_f", [P, CH])
        base_f = sb("base_f", [P, CH])
        span_f = sb("span_f", [P, CH])
        win_row = sb("win_row", [1, CH * P], I32)
        bank_row = sb("bank_row", [1, CH * P], I32)
        bank_f = sb("bank_f", [P, 3, CH])
        flag_f = sb("flag_f", [1, 1])
        flag_i = sb("flag_i", [1, 1], I32)
        iota = sb("iota", [P, SW])
        ident = sb("ident", [P, P])
        w_c = sb("w_c", [F, 2, F])
        w_g = sb("w_g", [F, 2, F])
        we_blk = sb("we_blk", [P, G * F])
        bias_b = sb("bias_b", [PN, 3, F])
        colv = sb("colv", [F, 4])
        deg = sb("deg", [PN, J])
        dinv = sb("dinv", [PN, J])
        stat = sb("stat", [PN, J, 6])
        nmean = sb("nmean", [PN, J])
        ssq = sb("ssq", [PN, J])
        rstd = sb("rstd", [PN, J])
        root_in = sb("root_in", [PN, J])
        root_out = sb("root_out", [PN, J])
        shift = sb("shift", [PN, J])
        tmp_j = sb("tmp_j", [PN, J])
        nmax = sb("nmax", [PN, J])
        esum = sb("esum", [PN, J])
        logz = sb("logz", [PN, J])
        degT = sb("degT", [P, CA, AL])
        idx = [sb(f"idx{u}", [P, G], I32) for u in range(U)]
        attr = [sb(f"attr{u}", [P, 3 * G]) for u in range(U)]
        rows_g = [sb(f"rows_g{u}", [P, G * F]) for u in range(U)]
        hot = [sb(f"hot{u}", [P, G, W]) for u in range(U)]
        ea = [sb(f"ea{u}", [P, G * KE]) for u in range(U)]
        eaT = sb("eaT", [P, U * P])
        t = DG * G
        deg_sets = [x_more_t[:, k * (AL + WA + WA * NB) * t // 2:(k + 1) * (AL + WA + WA * NB) * t // 2].bitcast(BF16) for k in range(DK)]
        hot_b = [v[:, 0:AL * t].rearrange("p (a t) -> p a t", t=t) for v in deg_sets]
        hot_a = [v[:, AL * t:(AL + WA) * t].rearrange("p (a t) -> p a t", t=t) for v in deg_sets]
        hot_w = [v[:, (AL + WA) * t:].rearrange("p (a k t) -> p a k t", k=NB, t=t) for v in deg_sets]
        zeros = sb("zeros", [P, BK], BF16)
        far = sb("far", [P, G, SW])
        far_i = sb("far_i", [P, 3, G], I32)
        far_c = sb("far_c", [P, 2, G])
        z1 = [far[0:F, k, :] for k in range(2)]
        bn = sb("bn", [F, NW, 6])
        bnv = sb("bnv", [F, 8])

        psum = ctx.enter_context(nc.psum_tensor("psum", [P, 8 * BK], F32))
        bank = [psum[:, k * BK:(k + 1) * BK] for k in range(8)]
        ps_agg = [bank[u][0:F, 0:W] for u in range(U)]
        ps_e = [bank[3 + u][:, 0:G * F] for u in range(U)]
        lin_bank = bank[0:3] + bank[5:8]
        LB = len(lin_bank)
        ps_t = bank[6][:, 0:U * P]
        ps_far = bank[7][0:F, 0:SW]
        ps_deg = psum[0:AL, 5 * BK:(5 + NB) * BK]
        ps_degf = bank[4][0:AL, 0:NA]

        s_dst, s_src, s_wgt = sem("dst_loaded"), sem("src_loaded"), sem("weight_loaded")
        s_x, s_par, s_blk = sem("x_loaded"), sem("params_loaded"), sem("we_loaded")
        s_const, s_blk0, s_zero = sem("constants_made"), sem("we_cleared"), sem("zeros_made")
        s_v = sem("vector_step")
        s_rows, s_tr, s_trc = sem("rows_ready"), sem("edges_transposed"), sem("edges_copied")
        s_trc_v = sem("edges_copied_vector")
        s_wt, s_flag = sem("windows_transposed"), sem("flag_ready")
        s_dhot, s_dsum, s_dall = sem("deg_hot_ready"), sem("deg_hot_used"), sem("deg_summed")
        s_dha, s_dhw = sem("deg_hot_a_ready"), sem("deg_hot_weighted")
        s_part, s_left = sem("weight_part_ready"), sem("weight_left")
        s_xln = sem("x_row_sums")
        s_dsb, s_dT, s_dc = sem("deg_in_sbuf"), sem("deg_transposed"), sem("deg_copied")
        s_dout, s_din = sem("deg_stored"), sem("deg_loaded")
        s_root, s_rooted = sem("root_wanted"), sem("root_done")
        s_tab, s_tabw = sem("table_chunk_ready"), sem("table_stored")
        s_nt, s_ntc = sem("nodes_transposed"), sem("nodes_copied")
        s_lin, s_linv, s_relu = sem("linear_done"), sem("linear_read"), sem("layer1_relu")
        s_relu_v = sem("layer1_relu_vector")
        s_exp, s_expd, s_ln, s_logz = sem("row_max_ready"), sem("exp_done"), sem("log_done"), sem("logz_ready")
        s_be = sem("gin_table_ready")
        s_ls = sem("log_softmax_ready")
        s_xm = [sem(f"x_chunk_loaded{k}") for k in range(2)]
        s_xt, s_sum, s_scale = sem("x_loaded_again"), sem("x_plus_z_ready"), sem("gin_scale_ready")
        s_norm, s_norm_v = sem("gin_rows_ready"), sem("gin_rows_ready_vector")
        s_cent, s_x1 = sem("rows_centred"), sem("x_plus_gcn_ready")
        s_m1, s_z1, s_m2, s_z2 = sem("mlp1_done"), sem("mlp1_relu"), sem("mlp2_done"), sem("mlp2_biased")
        s_bn, s_y = sem("bn_ready"), sem("bn_applied")
        s_yt, s_ya, s_out = sem("out_transposed"), sem("out_ready"), sem("out_stored")

        class Ring:

            def __init__(self, name, slots):
                self.slots = slots
                self.staged = sem(f"{name}_staged")
                self.issue = sem(f"{name}_issue")
                self.hot = sem(f"{name}_hot")
                self.agg = sem(f"{name}_agg")
                self.added = sem(f"{name}_added")
                self.ea = [sem(f"{name}_ea{u}") for u in range(slots)]
                self.tr = sem(f"{name}_ea_transposed")
                self.trc = sem(f"{name}_ea_copied")
                self.lin = sem(f"{name}_ea_linear")
                self.msg = sem(f"{name}_msg")
                self.relu = sem(f"{name}_relu")

        fast, slow = Ring("fast", U), Ring("slow", 1)
        fast_got = [sem(f"fast_gathered{u}") for u in range(U)]
        slow_got = [sem(f"slow_gathered{p}") for p in range(PASSES)]
        far_used = sem("far_used")
        far_moved = sem("far_moved")
        far_deg = sem("far_deg_step")
        far_dsum = sem("far_deg_used")
        USES = [ITERS + 1] + [ITERS] * (U - 1)

        def each_group(eng, body):
            with eng.Fori(0, ITERS) as it:
                for u in range(U):
                    body(it * U + u, it, u, P)
            body(FULL, ITERS, 0, TP)

        def if_far(eng, sweep):
            any_far = eng.value_load(flag_i[0:1, 0:1], min_val=0, max_val=1)
            with eng.If(any_far > 0):
                sweep()

        def each_slow(eng, body):
            with eng.Fori(0, FULL) as s:
                body(s, P)
            body(FULL, TP)

        def windows(eng, kind, first, k, of):
            return nc.values_load_multi_w_load_instructions(
                of[0:1, bass.ds(first, k)], engines=[kind], min_val=0,
                max_val=NA - 1 if of is win_row else (NB - 1) * BK + NB * (BA - 1),
                skip_runtime_bounds_check_because="a window starts at the least of its group's targets, which are nodes")[1]

        def by_group(t, s):
            return t[:, bass.ds(s, 1), :].rearrange("p s k -> p (s k)")

        def dve_norm(q):
            takes = lambda r: r >= CUTS[2] and r % 2 == 1
            return takes(q), sum(takes(r) for r in range(q + 1))

        def gin_steps(c):
            return range(CUTS[c], CUTS[c + 1])

        def gin_cols(c):
            return slice(CUTS[c] * JQ, CUTS[c + 1] * JQ)

        def x_more_cols(c):
            return slice(0, (CUTS[c + 1] - CUTS[c]) * JQ)

        def edge_list(n):
            c, k = divmod(n, 4)
            nq = P if c < CH - 1 else LASTQ
            return (edge[:, c * P:c * P + nq, k * G:(k + 1) * G],
                    bank[k][:, 0:G * nq].rearrange("p (g q) -> p q g", g=G))

        block = ctx.enter_context(nc.Block())

        @block.sync
        def _(sp):
            def load_rows(tile, dram, s):
                q = CH - 1
                n = q * P * GE
                end = FULL * GE
                sp.dma_start(tile[:, 0:q, :], dram[0:n].rearrange("(c q e) -> q c e", q=P, e=GE)).then_inc(s, 16)
                sp.dma_start(tile[0:LASTQ - 1, q, :], dram[n:end].rearrange("(q e) -> q e", e=GE)).then_inc(s, 16)
                sp.dma_start(tile[LASTQ - 1:LASTQ, q, 0:G * TP],
                             dram[end:E].rearrange("(a e) -> a e", a=1)).then_inc(s, 16)
                sp.dma_start(tile[LASTQ - 1:LASTQ, q, G * TP:GE],
                             dram[E - (GE - G * TP):E].rearrange("(a e) -> a e", a=1)).then_inc(s, 16)

            def node_dma(to_dram, dram, tile, c0, c1, s):
                d = dram.rearrange("(p j) f -> p j f", j=J)
                for a, b in ((0, PK), (PK, PN)):
                    there, here = d[a:b, c0:c1, :], tile[a:b, c0:c1, :]
                    sp.dma_start(*((there, here) if to_dram else (here, there))).then_inc(s, 16)

            load_rows(dst_i, dst, s_dst)
            load_rows(src_i, src, s_src)
            load_rows(row_wgt, edge_weight, s_wgt)
            node_dma(False, x, x_sb, 0, J, s_x)
            for t, w in ((w_c[:, 0, :], c1_w), (w_c[:, 1, :], c2_w), (w_g[:, 0, :], g1_w), (w_g[:, 1, :], g2_w)):
                sp.dma_start(t, w).then_inc(s_par, 16)
            for k, b in enumerate((c1_b, c2_b, be)):
                sp.dma_start(bias_b[:, k, :], b.rearrange("(a n) -> a n", a=1).to_broadcast([PN, F])).then_inc(s_par, 16)
            for k, b in enumerate((g1_b, g2_b, gamma, beta)):
                sp.dma_start(colv[:, k:k + 1], b.rearrange("(n a) -> n a", a=1)).then_inc(s_par, 16)
            sp.wait_ge(s_blk0, 1)
            for g in range(G):
                sp.dma_start(we_blk[KE * g:KE * g + KE, F * g:F * g + F], we).then_inc(s_blk, 16)

            sp.wait_ge(s_dc, CA)
            for c in range(CA):
                n = min(P, NA - c * P)
                sp.dma_start(deg_lin[c * P * AL:(c * P + n) * AL].rearrange("(q b) -> q b", b=AL),
                             degT[0:n, c, :]).then_inc(s_dout, 16)
            sp.wait_ge(s_dout, 16 * CA)
            sp.dma_start(deg[:, :], deg_lin[0:N].rearrange("(p j) -> p j", j=J)).then_inc(s_din, 16)

            def load_x_more(c):
                d = x.rearrange("(p j) f -> p j f", j=J)
                for a, b in ((0, PK), (PK, PN)):
                    sp.dma_start(x_more[a:b, c % 2, x_more_cols(c), :], d[a:b, gin_cols(c), :]).then_inc(s_xm[c % 2], 16)

            for p in range(PASSES):
                if p == 2:
                    for c in range(GC):
                        if c >= 2:
                            sp.wait_ge(s_sum, c - 1)
                        load_x_more(c)
                for c in range(GC if p == 2 else NC):
                    if p == 1:
                        sp.wait_ge(s_relu, ((c + 1) * QC + 1) // 2 * JQ)
                        sp.wait_ge(s_relu_v, (c + 1) * QC // 2)
                    elif p == 0:
                        sp.wait_ge(s_tab, c + 1)
                    else:
                        sp.wait_ge(s_be, c + 1)
                    cols = gin_cols(c) if p == 2 else slice(c * JC, (c + 1) * JC)
                    node_dma(True, table[p], tab, cols.start, cols.stop, s_tabw)

            sp.wait_ge(s_tabw, 32 * (2 * NC + GC))
            def load_ea(ring, s, u, np_):
                sp.wait_ge(ring.tr, s + 1)
                sp.dma_start(ea[u][0:np_, :],
                             edge_attr[bass.ds(s * GE, G * np_), :].rearrange("(p g) k -> p (g k)", g=G)
                             ).then_inc(ring.ea[u], 16)

            with sp.Fori(0, J) as it:
                for u in range(U):
                    load_ea(fast, it * U + u, u, P)
                sp.dma_start(tab[:, bass.ds(it, 1), :], x.rearrange("(p j) f -> p j f", j=J)[:, bass.ds(it, 1), :]).then_inc(s_xt, 16)
            with sp.Fori(J, ITERS) as it:
                for u in range(U):
                    load_ea(fast, it * U + u, u, P)
            load_ea(fast, FULL, 0, TP)

            def sweep():
                sp.wait_ge(fast.tr, NS + U)
                each_slow(sp, lambda s, np_: load_ea(slow, s, 0, np_))

            if_far(sp, sweep)

            for c in range(NC):
                sp.wait_ge(s_ya, (c + 1) * QC)
                node_dma(True, out, x_sb, c * JC, (c + 1) * JC, s_out)
            sp.wait_ge(s_out, 32 * NC)

        @block.gpsimd
        def _(pool):
            pool.memset(we_blk[:, :], 0.0).then_inc(s_blk0, 1)
            pool.iota(iota_i[:, :], pattern=[[1, SW]], base=0, channel_multiplier=0).then_inc(s_const, 1)
            pool.memset(ident[:, :], 0.0).then_inc(s_const, 1)
            pool.wait_ge(s_const, 2)
            pool.affine_select(out=ident[:, :], in_=ident[:, :], compare_op=ALU.not_equal, fill=1.0,
                               base=0, pattern=[[-1, P]], channel_multiplier=1).then_inc(s_const, 1)

            def gather(ring, p, s, u, np_, got):
                pool.wait_ge(ring.staged, p * NS + s + 1)
                pool.sem_inc(ring.issue, 1)
                for g in range(G):
                    pool.indirect_dma_start(
                        out=rows_g[u][0:np_, g * F:(g + 1) * F], out_offset=None, in_=table[p],
                        in_offset=bass.IndirectOffsetOnAxis(ap=idx[u][0:np_, g:g + 1], axis=0),
                    ).then_inc(got, 16)

            def centre(c):
                js = slice(c * JC, (c + 1) * JC)
                m = nmean[:, js].unsqueeze(2).to_broadcast([PN, JC, F])
                pool.tensor_tensor(tab[:, js, :], x_sb[:, js, :], m, ALU.add).then_inc(s_cent, 1)

            def add_x(c):
                js = gin_cols(c)
                pool.wait_ge(s_linv, J + js.stop)
                pool.wait_ge(s_xm[c % 2], 32 * (c // 2 + 1))
                pool.tensor_tensor(tab[:, js, :], x_sb[:, js, :], x_more[:, c % 2, x_more_cols(c), :], ALU.add).then_inc(s_sum, 1)

            def add_be(c):
                js = gin_cols(c)
                b = bias_b[:, 2, :].unsqueeze(1).to_broadcast([PN, js.stop - js.start, F])
                pool.wait_ge(s_nt, 2 * NQ + CUTS[c + 1])
                pool.tensor_tensor(tab[:, js, :], tab[:, js, :], b, ALU.add).then_inc(s_be, 1)

            pool.wait_ge(s_part, 1)
            v4 = lambda t: t.rearrange("p (s g) -> p s g", g=G)
            pool.tensor_tensor(v4(wgt_r), edge[:, :, 2 * G:3 * G], v4(wgt3[:, 0, :]), ALU.subtract).then_inc(s_left, 1)
            pool.wait_ge(s_left, 1)
            pool.wait_ge(s_part, 2)
            pool.tensor_tensor(wgt_r, wgt_r, wgt3[:, 1, :], ALU.subtract).then_inc(s_left, 1)
            pool.wait_ge(s_part, NB)

            def deg_weigh(n, s0, k, ng, np_):
                t = ng * G
                pool.wait_ge(s_dha, n + 1)
                a4 = hot_a[k][0:np_, :, 0:t].unsqueeze(2).to_broadcast([np_, WA, NB, t])
                w4 = wgt3[0:np_, :, bass.ds(s0 * G, t)].unsqueeze(1).to_broadcast([np_, WA, NB, t])
                pool.tensor_tensor(hot_w[k][0:np_, :, :, 0:t], a4, w4, ALU.mult).then_inc(s_dhw, 1)

            with pool.Fori(0, FULL // (DK * DG)) as it:
                for k in range(DK):
                    deg_weigh(it * DK + k, (it * DK + k) * DG, k, DG, P)
            deg_weigh(FULL // DG, FULL, 0, 1, TP)

            pool.wait_ge(s_par, 16 * 11)
            pool.wait_ge(s_tr, 4 * CH)
            for c in range(NC):
                pool.wait_ge(s_xln, (c + 1) * JC)
                centre(c)

            for p in range(PASSES):
                if p == 2:
                    for c in range(GC + 2):
                        if c < GC:
                            add_x(c)
                        if c >= 2:
                            add_be(c - 2)
                pool.wait_ge(s_tabw, 32 * ((p + 1) * NC if p < 2 else 2 * NC + GC))
                each_group(pool, lambda s, it, u, np_: gather(fast, p, s, u, np_, fast_got[u]))
                if_far(pool, lambda: each_slow(pool, lambda s, np_: gather(slow, p, s, 0, np_, slow_got[p])))

            pool.wait_ge(s_xt, 16 * J)
            pool.wait_ge(s_logz, 1)
            for c in range(NC):
                js = slice(c * JC, (c + 1) * JC)
                lz = logz[:, js].unsqueeze(2).to_broadcast([PN, JC, F])
                pool.tensor_tensor(x_sb[:, js, :], x_sb[:, js, :], lz, ALU.subtract).then_inc(s_ls, 1)
                pool.wait_ge(s_ls, c + 1)
                pool.tensor_tensor(x_sb[:, js, :], x_sb[:, js, :], tab[:, js, :], ALU.add).then_inc(s_x1, 1)

        @block.scalar
        def _(act):
            act.sem_inc(fast.trc, U)
            act.sem_inc(slow.trc, 1)

            for n in range(0, 4 * CH, 2):
                act.wait_ge(s_tr, n + 1)
                act.activation(*edge_list(n), ACT.Copy).then_inc(s_trc, 1)

            act.wait_ge(s_trc, 2 * CH)
            v4 = lambda t: t.rearrange("p (s g) -> p s g", g=G)
            act.activation(v4(wgt3[:, 0, :]), edge[:, :, 2 * G:3 * G], ACT.Copy).then_inc(s_part, 1)
            for k in range(1, NB):
                act.wait_ge(s_left, k)
                act.activation(wgt3[:, k, :], wgt_r, ACT.Copy).then_inc(s_part, 1)

            act.wait_ge(s_x, 32)
            DUMP = U * G
            for k in range(2 * J):
                j, d = k % J, k % DUMP
                o = rows_g[d // G][0:PN, d % G * F:(d % G + 1) * F]
                if k >= DUMP:
                    act.wait_ge(s_xln, k - DUMP + 1)
                if k < J:
                    act.activation(o, x_sb[:, j, :], ACT.Copy, scale=-1.0 / F, accum_out=nmean[:, j:j + 1]).then_inc(s_xln, 1)
                else:
                    act.activation(o, x_sb[:, j, :], ACT.Square, bias=nmean[:, j:j + 1], accum_out=ssq[:, j:j + 1]).then_inc(s_xln, 1)

            def root(n, o, i):
                act.wait_ge(s_root, n + 1)
                act.activation(o, i, ACT.Sqrt).then_inc(s_rooted, 1)

            def copy_nodes(p, q):
                act.wait_ge(s_nt, p * NQ + q + 1)
                act.activation(acc_j[:, q * JQ:(q + 1) * JQ, :],
                               bank[3 + q % 2][0:F, 0:JQ * PN].rearrange("f (j p) -> f j p", j=JQ),
                               ACT.Copy).then_inc(s_ntc, 1)

            def stage(ring, p, s, u, np_):
                e = by_group(edge[0:np_, :, :], s)
                act.activation(attr[u][0:np_, :], e[:, G:4 * G], ACT.Copy)
                act.activation(idx[u][0:np_, :], e[:, 0:G], ACT.Copy).then_inc(ring.staged, 1)

            def stage_fast(p, s, u, np_):
                act.wait_ge(fast.agg, p * NS + s + 1)
                stage(fast, p, s, u, np_)

            def stage_slow(p, s, np_):
                act.wait_ge(slow.added, (p * NS + s) * NW + 1)
                stage(slow, p, s, 0, np_)

            def copy_eaT(ring, s, k, np_):
                act.wait_ge(ring.tr, s + k + ring.slots)
                act.wait_ge(ring.lin, s + ring.slots)
                w = (k - 1) * P + np_
                act.activation(eaT[:, 0:w], ps_t[:, 0:w], ACT.Copy).then_inc(ring.trc, k)

            def relu_msg(ring, s, u, np_):
                act.wait_ge(ring.msg, s + 1 + ring.slots)
                act.activation(rows_g[u][0:np_, :], rows_g[u][0:np_, :], ACT.Relu).then_inc(ring.relu, 1)

            def sweep(p):
                def one(s, np_):
                    stage_slow(p, s, np_)
                    if p == 2:
                        copy_eaT(slow, s, 1, np_)
                        relu_msg(slow, s, 0, np_)
                act.wait_ge(fast.agg, U + (p + 1) * NS)
                each_slow(act, one)

            root(0, root_out[:, :], root_in[:, :])
            root(1, root_out[:, :], root_in[:, :])
            act.wait_ge(s_trc_v, 2 * CH)
            for q in range(NQ):
                copy_nodes(0, q)
            each_group(act, lambda s, it, u, np_: stage_fast(0, s, u, np_))
            if_far(act, lambda: sweep(0))

            LAG = 3
            for q in range(NQ + LAG):
                if q < NQ and q % 2 == 0:
                    for j in range(q * JQ, (q + 1) * JQ):
                        act.wait_ge(s_linv, j + 1)
                        act.activation(tab[:, j, :], tab[:, j, :], ACT.Relu, scale=dinv[:, j:j + 1]).then_inc(s_relu, 1)
                if q >= LAG:
                    copy_nodes(1, q - LAG)
            act.wait_ge(fast.agg, U + NS)
            each_group(act, lambda s, it, u, np_: stage_fast(1, s, u, np_))
            if_far(act, lambda: sweep(1))

            for c in range(GC + 1):
                if c < GC:
                    cc = gin_cols(c)
                    root(2 + c, root_out[:, cc], root_in[:, cc])
                if c >= 1:
                    for q in gin_steps(c - 1):
                        copy_nodes(2, q)
                if c < GC:
                    act.wait_ge(s_scale, c + 1)
                    for q in gin_steps(c):
                        if dve_norm(q)[0]:
                            continue
                        for j in range(q * JQ, (q + 1) * JQ):
                            last = act.activation(tab[:, j, :], tab[:, j, :], ACT.Relu, scale=rstd[:, j:j + 1], bias=shift[:, j:j + 1])
                        last.then_inc(s_norm, 1)

            act.wait_ge(fast.agg, U + 2 * NS)
            for u in range(U):
                stage_fast(2, u, u, P)

            def exp_sum(j):
                act.wait_ge(s_exp, j + 1)
                act.wait_ge(s_expd, j + 1)
                act.activation(x_more[:, 0, 0, :], x_sb[:, bass.ds(j, 1), :].rearrange("p a f -> p (a f)"), ACT.Exp,
                               bias=nmax[:, bass.ds(j, 1)], accum_out=esum[:, bass.ds(j, 1)]).then_inc(s_expd, 1)

            def gin_body(s0, last):
                copy_eaT(fast, s0, U, P)
                for u in range(U):
                    relu_msg(fast, s0 + u, u, P)
                    if not last:
                        stage_fast(2, s0 + U + u, u, P)
                    elif u == 0:
                        stage_fast(2, FULL, 0, TP)

            act.sem_inc(s_expd, 1)
            exp_sum(0)
            with act.Fori(1, J) as it:
                gin_body((it - 1) * U, False)
                exp_sum(it)
            gin_body((J - 1) * U, False)
            with act.Fori(J, ITERS - 1) as it:
                gin_body(it * U, False)
            gin_body(FULL - U, True)
            copy_eaT(fast, FULL, 1, TP)
            relu_msg(fast, FULL, 0, TP)
            act.wait_ge(s_expd, J + 1)
            act.activation(esum[:, :], esum[:, :], ACT.Ln).then_inc(s_ln, 1)
            if_far(act, lambda: sweep(2))

            for w in range(NW):
                act.wait_ge(s_m1, w + 1)
                act.activation(z1[w % 2], bank[w % 2][0:F, 0:SW], ACT.Relu, bias=colv[:, 0:1]).then_inc(s_z1, 1)
                if w >= 1:
                    act.wait_ge(s_m2, w)
                    act.activation(acc[:, (w - 1) * SW:w * SW], bank[2 + (w - 1) % 2][0:F, 0:SW], ACT.Identity,
                                   bias=colv[:, 1:2]).then_inc(s_z2, 1)
            act.wait_ge(s_m2, NW)
            act.activation(acc[:, (NW - 1) * SW:N], bank[2 + (NW - 1) % 2][0:F, 0:SW], ACT.Identity,
                           bias=colv[:, 1:2]).then_inc(s_z2, 1)
            root(2 + GC, bnv[:, 3:4], bnv[:, 2:3])
            act.wait_ge(s_bn, 1)
            for c in range(NC):
                a = acc_t[0:F, 0:N].rearrange("f (p j) -> f p j", j=J)[:, :, c * JC:(c + 1) * JC]
                act.activation(a, a, ACT.Relu, scale=bnv[:, 6:7], bias=bnv[:, 7:8]).then_inc(s_y, 1)

        @block.tensor
        def _(pe):
            for r, n in ((fast, U), (slow, 1)):
                pe.sem_inc(r.agg, n)
                pe.sem_inc(r.tr, n)
                pe.sem_inc(r.lin, n)
            pe.sem_inc(far_used, 1)
            pe.sem_inc(far_dsum, 1)
            pe.sem_inc(s_dsum, DK)

            pe.wait_ge(s_const, 3)
            pe.wait_ge(s_rows, 1)
            pe.wait_ge(s_wgt, 64)
            def bank_free(n):
                if n >= 4:
                    pe.wait_ge(s_trc_v if n % 2 else s_trc, (n - 4) // 2 + 1)
            for n in range(4 * CH):
                c, k = divmod(n, 4)
                nq = P if c < CH - 1 else LASTQ
                bank_free(n)
                for g in range(G):
                    last = pe.transpose(bank[n % 4][:, g * nq:(g + 1) * nq], row[k][0:nq, c, g:GE:G], ident[0:nq, 0:nq])
                last.then_inc(s_tr, 1)
            for n in range(4 * CH, 4 * CH + 3):
                bank_free(n)
            for c in range(CH):
                for k, t in enumerate((win_f[:, c:c + 1], bank_f[:, 0, c:c + 1], span_f[:, c:c + 1])):
                    last = pe.transpose(bank[k][0:1, c * P:(c + 1) * P], t, ident[:, :])
            last.then_inc(s_wt, 1)

            def zero_deg(first):
                pe.matmul(ps_degf, zeros[:, 0:AL], zeros[:, 0:NA], start=first, stop=not first)
                for k in range(NB):
                    last = pe.matmul(ps_deg[:, k * BK:k * BK + NB * (BA + WA)], zeros[:, 0:AL],
                                     zeros[:, 0:NB * (BA + WA)], start=first, stop=not first)
                return last

            pe.wait_ge(s_zero, 1)
            zero_deg(True)
            pe.wait_ge(s_flag, 1)

            def deg_step(n, w, k, np_):
                pe.wait_ge(s_dhot, n + 1)
                pe.wait_ge(s_dhw, n + 1)
                for i in range(len(w)):
                    for g in range(G):
                        t = i * G + g
                        last = pe.matmul(ps_deg[:, bass.ds(w[i], WA * NB)], hot_b[k][0:np_, :, t],
                                         hot_w[k][0:np_, :, :, t].rearrange("p a k -> p (a k)"), start=False, stop=False)
                last.then_inc(s_dsum, 1)

            with pe.Fori(0, FULL // (DK * DG)) as it:
                w = windows(pe, mybir.EngineType.PE, it * DK * DG, DK * DG, bank_row)
                for k in range(DK):
                    deg_step(it * DK + k, w[k * DG:(k + 1) * DG], k, P)
            deg_step(FULL // DG, windows(pe, mybir.EngineType.PE, FULL, 1, bank_row), 0, TP)

            def deg_sweep():
                def one(s, np_):
                    pe.wait_ge(far_deg, 6 * s + 6)
                    for g in range(G):
                        last = pe.matmul(ps_degf, hot[0][0:np_, g, 0:AL], far[0:np_, g, 0:NA],
                                         start=False, stop=False)
                    last.then_inc(far_dsum, 1)
                each_slow(pe, one)

            if_far(pe, deg_sweep)
            zero_deg(False).then_inc(s_dall, 1)
            pe.wait_ge(s_dsb, 1)
            for c in range(CA):
                n = min(P, NA - c * P)
                last = pe.transpose(bank[2][0:n, c * AL:(c + 1) * AL], deg_sb[:, c * P:c * P + n], ident[0:AL, 0:AL])
            last.then_inc(s_dT, 1)

            def transpose_nodes(p, q):
                if q >= 2:
                    pe.wait_ge(s_ntc, p * NQ + q - 1)
                for i in range(JQ):
                    last = pe.transpose(bank[3 + q % 2][0:F, i * PN:(i + 1) * PN], tab[:, q * JQ + i, :], ident[0:PN, 0:PN])
                last.then_inc(s_nt, 1)

            def transpose_ea(ring, s, first, it, u, np_):
                pe.wait_ge(ring.ea[u], 16 * (it + 1))
                pe.wait_ge(ring.trc, first + ring.slots)
                pe.transpose(ps_t[:, u * P:u * P + np_], ea[u][0:np_, :], ident[0:np_, 0:np_]).then_inc(ring.tr, 1)

            def linear_ea(ring, s, upto, u, np_):
                pe.wait_ge(ring.trc, upto + ring.slots)
                pe.wait_ge(ring.msg, s + 1)
                pe.matmul(ps_e[u][0:np_, :], eaT[:, u * P:u * P + np_], we_blk[:, :], start=True, stop=True).then_inc(ring.lin, 1)

            def aggregate(p, s, it, u, np_):
                n = p * NS + s
                pe.wait_ge(fast.hot, n + 1)
                pe.wait_ge(fast.added, n + 1)
                if p < 2:
                    pe.wait_ge(fast_got[u], 16 * G * (p * USES[u] + it + 1))
                else:
                    pe.wait_ge(fast.relu, s + 1)
                for g in range(G):
                    last = pe.matmul(ps_agg[u], rows_g[u][0:np_, g * F:(g + 1) * F], hot[u][0:np_, g, :],
                                     start=g == 0, stop=g == G - 1)
                last.then_inc(fast.agg, 1)

            def sweep(p):
                def one(s, np_):
                    n = p * NS + s
                    if p == 2:
                        transpose_ea(slow, s, s, s, 0, np_)
                        linear_ea(slow, s, s + 1, 0, np_)
                    with pe.Fori(0, NW) as w:
                        if p == 2:
                            pe.wait_ge(slow.relu, s + 1)
                        else:
                            pe.wait_ge(slow_got[p], 16 * G * (s + 1))
                        pe.wait_ge(slow.hot, n * NW + w + 1)
                        pe.wait_ge(slow.added, n * NW + w + 1)
                        for g in range(G):
                            last = pe.matmul(ps_far, rows_g[0][0:np_, g * F:(g + 1) * F], far[0:np_, g, :],
                                             start=g == 0, stop=g == G - 1)
                        last.then_inc(far_used, 1)
                each_slow(pe, one)
                pe.wait_ge(slow.added, (p + 1) * NS * NW + 1)

            def warm(n):
                for _ in range(n):
                    pe.matmul(ps_far, zeros[:, 0:F], zeros[:, 0:SW], start=True, stop=True)

            def linear(p, q):
                if q >= LB:
                    pe.wait_ge(s_linv, p * J + (q - LB + 1) * JQ)
                for i in range(JQ):
                    last = pe.matmul(lin_bank[q % LB][0:PN, i * F:(i + 1) * F], acc_j[:, q * JQ + i, :], w_c[:, p, :],
                                     start=True, stop=True)
                last.then_inc(s_lin, 1)

            for c in range(NC):
                pe.wait_ge(s_tab, c + 1)
                for q in range(c * QC, (c + 1) * QC):
                    transpose_nodes(0, q)
            with pe.Fori(0, ITERS) as it:
                for u in range(U):
                    aggregate(0, it * U + u, it, u, P)
            warm(WARM)
            aggregate(0, FULL, ITERS, 0, TP)
            pe.wait_ge(fast.added, U + NS)
            if_far(pe, lambda: sweep(0))

            pe.wait_ge(s_par, 16 * 11)
            LAG = 3
            for q in range(NQ + LAG):
                if q < NQ:
                    linear(0, q)
                if q >= LAG:
                    if (q - LAG) % 2 == 0:
                        pe.wait_ge(s_relu, ((q - LAG) // 2 + 1) * JQ)
                    else:
                        pe.wait_ge(s_relu_v, (q - LAG + 1) // 2)
                    transpose_nodes(1, q - LAG)
            with pe.Fori(0, ITERS) as it:
                for u in range(U):
                    aggregate(1, it * U + u, it, u, P)
            warm(WARM)
            aggregate(1, FULL, ITERS, 0, TP)
            pe.wait_ge(fast.added, U + 2 * NS)
            if_far(pe, lambda: sweep(1))

            AHEAD = 3
            for c in range(GC + AHEAD):
                if c < GC:
                    for q in gin_steps(c):
                        linear(1, q)
                if c >= AHEAD:
                    for q in gin_steps(c - AHEAD):
                        takes, n = dve_norm(q)
                        if takes:
                            pe.wait_ge(s_norm_v, n)
                        else:
                            pe.wait_ge(s_norm, q + 1 - n)
                        transpose_nodes(2, q)

            pe.wait_ge(s_blk, 16 * G)
            def gin_body(s0, it):
                for u in range(U):
                    transpose_ea(fast, s0 + u, s0, it, u, P)
                for u in range(U):
                    linear_ea(fast, s0 + u, s0 + U, u, P)
                for u in range(U):
                    aggregate(2, s0 + u, it, u, P)
            with pe.Fori(0, ITERS) as it:
                gin_body(it * U, it)
            transpose_ea(fast, FULL, FULL, ITERS, 0, TP)
            linear_ea(fast, FULL, NS, 0, TP)
            aggregate(2, FULL, ITERS, 0, TP)
            pe.wait_ge(fast.added, U + 3 * NS)
            if_far(pe, lambda: sweep(2))

            for w in range(NW + 1):
                if w < NW:
                    if w >= 2:
                        pe.wait_ge(s_z1, w - 1)
                    pe.matmul(bank[w % 2][0:F, 0:SW], w_g[:, 0, :], acc[:, w * SW:(w + 1) * SW],
                              start=True, stop=True).then_inc(s_m1, 1)
                if w >= 1:
                    v = w - 1
                    pe.wait_ge(s_z1, w)
                    if v >= 2:
                        pe.wait_ge(s_z2, v - 1)
                    pe.matmul(bank[2 + v % 2][0:F, 0:SW], w_g[:, 1, :], z1[v % 2],
                              start=True, stop=True).then_inc(s_m2, 1)
            for q in range(NQ):
                pe.wait_ge(s_y, q // QC + 1)
                if q >= 3:
                    pe.wait_ge(s_ya, q - 2)
                for i in range(JQ):
                    last = pe.transpose(bank[4 + q % 3][0:PN, i * F:(i + 1) * F], acc_j[:, q * JQ + i, :], ident[0:F, 0:F])
                last.then_inc(s_yt, 1)

        @block.vector
        def _(dve):
            for r, n in ((fast, U), (slow, 1)):
                dve.sem_inc(r.added, n)
                dve.sem_inc(r.msg, n)

            steps = [0]

            def then(ins):
                steps[0] += 1
                ins.then_inc(s_v, 1)
                dve.wait_ge(s_v, steps[0])

            def parts(f):
                f(slice(0, P), slice(0, CH - 1))
                return f(slice(0, LASTQ), slice(CH - 1, CH))

            dve.memset(acc_t[:, N:], 0.0)
            dve.memset(win_f[:, :], 0.0)
            dve.memset(bank_f[:, :, :], 0.0)
            then(dve.memset(span_f[:, :], 0.0))
            dve.memset(zeros[:, :], 0.0).then_inc(s_zero, 1)
            dve.wait_ge(s_const, 3)
            then(dve.tensor_copy(iota[:, :], iota_i[:, :]))
            dve.tensor_copy(iota_b[:, :, :], iota[:, 0:AL].unsqueeze(2).to_broadcast([P, AL, DG * G]))

            dve.wait_ge(s_dst, 64)
            then(parts(lambda q, c: dve.tensor_copy(row_dst[q, c, :], dst_i[q, c, :])))
            parts(lambda q, c: dve.tensor_reduce(least[q, c], row_dst[q, c, :], AX.X, ALU.min))
            then(parts(lambda q, c: dve.tensor_reduce(most[q, c], row_dst[q, c, :], AX.X, ALU.max)))
            then(parts(lambda q, c: dve.tensor_copy(base_i[q, c], least[q, c])))
            then(parts(lambda q, c: dve.tensor_single_scalar(win_i[q, c], base_i[q, c], 5, ALU.arith_shift_right)))
            then(parts(lambda q, c: dve.tensor_copy(win_f[q, c], win_i[q, c])))
            for k in range(1, NB):
                parts(lambda q, c: dve.tensor_scalar(bank_f[q, k, c], win_f[q, c], float(k * BA), float(BK - NB * BA), ALU.is_ge, ALU.mult))
            parts(lambda q, c: dve.tensor_scalar(bank_f[q, 0, c], win_f[q, c], float(NB), None, ALU.mult))
            then(parts(lambda q, c: dve.tensor_scalar(base_f[q, c], win_f[q, c], float(AL), None, ALU.mult)))
            then(parts(lambda q, c: dve.tensor_tensor(bank_f[q, 0, c], bank_f[q, 0, c], bank_f[q, 1, c], ALU.add)))
            parts(lambda q, c: dve.tensor_tensor(bank_f[q, 0, c], bank_f[q, 0, c], bank_f[q, 2, c], ALU.add))
            parts(lambda q, c: dve.tensor_tensor(span_f[q, c], most[q, c], base_f[q, c], ALU.subtract))
            for c in range(CH):
                q = slice(0, P if c < CH - 1 else LASTQ)
                last = dve.tensor_scalar(row_rel[q, c, :], row_dst[q, c, :], base_f[q, c:c + 1], None, ALU.subtract)
            then(last)
            then(parts(lambda q, c: dve.tensor_scalar(row_far[q, c, :], row_rel[q, c, :], float(W), FAR, ALU.is_lt, ALU.mult)))
            parts(lambda q, c: dve.tensor_tensor(row_far[q, c, :], row_far[q, c, :], row_dst[q, c, :], ALU.add))
            dve.wait_ge(s_src, 64)
            parts(lambda q, c: dve.tensor_copy(row_src[q, c, :], src_i[q, c, :])).then_inc(s_rows, 1)
            for n in range(1, 4 * CH, 2):
                dve.wait_ge(s_tr, n + 1)
                dve.tensor_copy(*edge_list(n)).then_inc(s_trc_v, 1)

            def ln_stats(c):
                for j in range(gin_cols(c).start, gin_cols(c).stop):
                    last = dve.bn_stats(stat[:, j, :], tab[:, j, :])
                return last

            def ln_rstd_start(js):
                me, mo, ve, vo = (stat[:, js, k] for k in (1, 4, 2, 5))
                m, r, t = nmean[:, js], root_in[:, js], tmp_j[:, js]
                dve.tensor_tensor(m, me, mo, ALU.add)
                dve.tensor_tensor(t, me, mo, ALU.subtract)
                then(dve.tensor_tensor(r, ve, vo, ALU.add))
                dve.tensor_scalar(m, m, -0.5, None, ALU.mult)
                then(dve.tensor_tensor(t, t, t, ALU.mult))
                then(dve.tensor_scalar(r, r, 1.0 / F, EPS, ALU.mult, ALU.add))
                dve.scalar_tensor_tensor(r, t, 0.25, r, ALU.mult, ALU.add).then_inc(s_root, 1)

            dve.wait_ge(s_trc_v, 2 * CH)
            v3 = lambda t: t.rearrange("p (s g) -> p s g", g=G)
            then(dve.tensor_copy(v3(col_i), edge[:, :, G:2 * G]))
            then(dve.tensor_single_scalar(col_i2, col_i, AL - 1, ALU.bitwise_and))
            dve.tensor_copy(col_b, col_i2)
            then(dve.tensor_single_scalar(col_i, col_i, 5, ALU.arith_shift_right))
            dve.tensor_copy(col_a, col_i)

            dve.wait_ge(s_wt, 1)
            dve.tensor_copy(bank_row[0:1, :], bank[1][0:1, 0:CH * P])
            dve.tensor_copy(win_row[0:1, :], bank[0][0:1, 0:CH * P])
            then(dve.tensor_reduce(flag_f[0:1, :], bank[2][0:1, 0:CH * P], AX.X, ALU.max))
            then(dve.tensor_scalar(flag_i[0:1, :], flag_f[0:1, :], float(W), None, ALU.is_ge))
            dve.sem_inc(s_flag, 1)

            def deg_hot(n, s0, k, ng, np_):
                t = ng * G
                cols = lambda a: a[0:np_, bass.ds(s0 * G, t)].unsqueeze(1)
                dve.wait_ge(s_dsum, n + 1)
                dve.tensor_tensor(hot_a[k][0:np_, :, 0:t], iota_b[0:np_, 0:WA, 0:t],
                                  cols(col_a).to_broadcast([np_, WA, t]), ALU.is_equal).then_inc(s_dha, 1)
                dve.tensor_tensor(hot_b[k][0:np_, :, 0:t], iota_b[0:np_, :, 0:t],
                                  cols(col_b).to_broadcast([np_, AL, t]), ALU.is_equal).then_inc(s_dhot, 1)

            with dve.Fori(0, FULL // (DK * DG)) as it:
                for k in range(DK):
                    deg_hot(it * DK + k, (it * DK + k) * DG, k, DG, P)
            deg_hot(FULL // DG, FULL, 0, 1, TP)

            def deg_sweep():
                dve.wait_ge(s_dsum, FULL // DG + 1 + DK)
                def one(s, np_):
                    k = 6 * s
                    o = slice(0, np_)
                    dve.wait_ge(far_dsum, s + 1)
                    dve.tensor_copy(far_i[o, 0, :], by_group(edge[o, :, :], s)[:, 3 * G:4 * G]).then_inc(far_deg, 1)
                    dve.wait_ge(far_deg, k + 1)
                    dve.tensor_single_scalar(far_i[o, 1, :], far_i[o, 0, :], AL - 1, ALU.bitwise_and).then_inc(far_deg, 1)
                    dve.tensor_single_scalar(far_i[o, 2, :], far_i[o, 0, :], 5, ALU.arith_shift_right).then_inc(far_deg, 1)
                    dve.wait_ge(far_deg, k + 3)
                    dve.tensor_copy(far_c[o, :, :], far_i[o, 1:3, :]).then_inc(far_deg, 1)
                    dve.tensor_copy(attr[0][o, 0:G], by_group(edge[o, :, :], s)[:, 2 * G:3 * G]).then_inc(far_deg, 1)
                    dve.wait_ge(far_deg, k + 5)
                    for g in range(G):
                        dve.tensor_scalar(hot[0][o, g, 0:AL], iota[o, 0:AL], far_c[o, 0, g:g + 1], None, ALU.is_equal)
                        last = dve.tensor_scalar(far[o, g, 0:NA], iota[o, 0:NA], far_c[o, 1, g:g + 1],
                                                 attr[0][o, g:g + 1], ALU.is_equal, ALU.mult)
                    last.then_inc(far_deg, 1)
                each_slow(dve, one)

            if_far(dve, deg_sweep)
            then(dve.memset(deg_sb, 0.0))
            dve.wait_ge(s_dall, 1)
            dve.tensor_copy(deg_sb[:, 0:NA], ps_degf)
            for k in range(NB):
                last = dve.tensor_reduce(deg_k[:, k * (BA + WA):(k + 1) * (BA + WA)],
                                         ps_deg[:, k * BK:k * BK + NB * (BA + WA)].rearrange("b (a k) -> b a k", k=NB), AX.X, ALU.add)
            then(last)
            for k in range(NB):
                a = deg_sb[:, k * BA:(k + 1) * BA + WA]
                last = dve.tensor_tensor(a, a, deg_k[:, k * (BA + WA):(k + 1) * (BA + WA)], ALU.add)
                if k < NB - 1:
                    then(last)
            last.then_inc(s_dsb, 1)
            dve.wait_ge(s_dT, 1)
            for c in range(CA):
                n = min(P, NA - c * P)
                dve.tensor_copy(degT[0:n, c, :], bank[2][0:n, c * AL:(c + 1) * AL]).then_inc(s_dc, 1)
            dve.wait_ge(s_xln, 2 * J)
            dve.tensor_scalar(root_in[:, :], ssq[:, :], 1.0 / F, EPS, ALU.mult, ALU.add).then_inc(s_root, 1)
            dve.wait_ge(s_rooted, 1)
            then(dve.reciprocal(rstd[:, :], root_out[:, :]))
            dve.wait_ge(s_din, 16)
            then(dve.tensor_scalar(deg[:, :], deg[:, :], 1.0, None, ALU.add))
            dve.tensor_scalar(root_in[:, :], deg[:, :], TINY, None, ALU.max).then_inc(s_root, 1)
            dve.tensor_scalar(tmp_j[:, :], deg[:, :], 0.0, None, ALU.is_gt)
            dve.wait_ge(s_rooted, 2)
            then(dve.reciprocal(dinv[:, :], root_out[:, :]))
            then(dve.tensor_tensor(dinv[:, :], dinv[:, :], tmp_j[:, :], ALU.mult))
            then(dve.tensor_tensor(tmp_j[:, :], dinv[:, :], rstd[:, :], ALU.mult))

            def chunk(t, c):
                return t[:, c * JC:(c + 1) * JC, :]

            def bc(t, c):
                return t[:, c * JC:(c + 1) * JC].unsqueeze(2).to_broadcast([PN, JC, F])

            for c in range(NC):
                dve.wait_ge(s_cent, c + 1)
                dve.scalar_tensor_tensor(chunk(tab, c), chunk(tab, c), 0.0, bc(tmp_j, c), ALU.max, ALU.mult).then_inc(s_tab, 1)

            def build_hot(p, s, u, np_):
                dve.wait_ge(fast.staged, p * NS + s + 1)
                for g in range(G):
                    rel = attr[u][0:np_, g:g + 1]
                    if p < 2:
                        last = dve.tensor_scalar(hot[u][0:np_, g, :], iota[0:np_, 0:W], rel,
                                                 attr[u][0:np_, G + g:G + g + 1], ALU.is_equal, ALU.mult)
                    else:
                        last = dve.tensor_scalar(hot[u][0:np_, g, :], iota[0:np_, 0:W], rel, None, ALU.is_equal)
                last.then_inc(fast.hot, 1)

            def add_window(p, s, u, w0):
                n = p * NS + s
                dve.wait_ge(fast.agg, n + 1 + U)
                dve.wait_ge(fast.added, n + U)
                a = acc[:, bass.ds(w0 * AL, W)]
                dve.tensor_tensor(a, a, ps_agg[u], ALU.add).then_inc(fast.added, 1)

            def add_edge_term(ring, s, it, u, np_):
                dve.wait_ge(ring.lin, s + 1 + ring.slots)
                if ring is fast:
                    dve.wait_ge(fast_got[u], 16 * G * (2 * USES[u] + it + 1))
                else:
                    dve.wait_ge(slow_got[2], 16 * G * (s + 1))
                r = rows_g[u][0:np_, :]
                dve.tensor_tensor(r, r, ps_e[u][0:np_, :], ALU.add).then_inc(ring.msg, 1)

            def row_max(j):
                c = bass.ds(j, 1)
                dve.tensor_reduce(nmax[:, c], x_sb[:, c, :], AX.X, ALU.max, negate=True).then_inc(s_exp, 1)

            def fast_pass(p):
                def body(it, us, np_, w):
                    s0 = it * U if us > 1 else FULL
                    for u in range(us):
                        build_hot(p, s0 + u, u, np_)
                    for u in range(us):
                        if p == 2:
                            add_edge_term(fast, s0 + u, it, u, np_)
                            if u >= 1:
                                add_window(p, s0 + u - 1, u - 1, w[u - 1])
                        else:
                            add_window(p, s0 + u, u, w[u])
                    if p == 2:
                        add_window(p, s0 + us - 1, us - 1, w[us - 1])
                dve.wait_ge(s_ntc, (p + 1) * NQ)
                def full(it):
                    body(it, U, P, windows(dve, mybir.EngineType.DVE, it * U, U, win_row))

                if p == 2:
                    row_max(0)
                    with dve.Fori(0, J - 1) as it:
                        row_max(it + 1)
                        full(it)
                with dve.Fori(J - 1 if p == 2 else 0, ITERS) as it:
                    full(it)
                body(ITERS, 1, TP, windows(dve, mybir.EngineType.DVE, FULL, 1, win_row))

            def sweep(p):
                def one(s, np_):
                    n = p * NS + s
                    o = slice(0, np_)
                    if p == 2:
                        add_edge_term(slow, s, s, 0, np_)
                    with dve.Fori(0, NW) as w:
                        m = n * NW + w
                        dve.wait_ge(slow.staged, n + 1)
                        dve.wait_ge(far_used, m + 1)
                        dve.wait_ge(far_moved, m + 1)
                        for g in range(G):
                            tgt = attr[0][o, 2 * G + g:2 * G + g + 1]
                            if p < 2:
                                last = dve.tensor_scalar(far[o, g, :], iota[o, :], tgt, attr[0][o, G + g:G + g + 1],
                                                         ALU.is_equal, ALU.mult)
                            else:
                                last = dve.tensor_scalar(far[o, g, :], iota[o, :], tgt, None, ALU.is_equal)
                        last.then_inc(slow.hot, 1)
                        dve.wait_ge(slow.hot, m + 1)
                        t = attr[0][o, 2 * G:3 * G]
                        dve.tensor_scalar(t, t, -float(SW), None, ALU.add).then_inc(far_moved, 1)
                        dve.wait_ge(far_used, m + 2)
                        dve.wait_ge(slow.added, m + 1)
                        a = acc[:, bass.ds(w * SW, SW)]
                        dve.tensor_tensor(a, a, ps_far, ALU.add).then_inc(slow.added, 1)
                dve.wait_ge(fast.added, U + (p + 1) * NS)
                if p == 0:
                    dve.sem_inc(far_moved, 1)
                each_slow(dve, one)

            def linear_read(p, q):
                dve.wait_ge(s_lin, p * NQ + q + 1)
                for i in range(JQ):
                    j = q * JQ + i
                    last = dve.scalar_tensor_tensor((x_sb if p else tab)[:, j, :], lin_bank[q % LB][0:PN, i * F:(i + 1) * F], dinv[:, j:j + 1],
                                                    bias_b[:, p, :], ALU.mult, ALU.add).then_inc(s_linv, 1)

            fast_pass(0)
            if_far(dve, lambda: sweep(0))
            dve.wait_ge(s_par, 16 * 11)
            dve.wait_ge(s_tabw, 32 * NC)
            for q in range(NQ):
                linear_read(0, q)
                if q % 2:
                    t = tab[:, q * JQ:(q + 1) * JQ, :]
                    dve.wait_ge(s_linv, (q + 1) * JQ)
                    dve.scalar_tensor_tensor(t, t, 0.0, dinv[:, q * JQ:(q + 1) * JQ].unsqueeze(2).to_broadcast([PN, JQ, F]),
                                             ALU.max, ALU.mult).then_inc(s_relu_v, 1)
            fast_pass(1)
            if_far(dve, lambda: sweep(1))

            def finish(c):
                js = gin_cols(c)
                dve.wait_ge(s_rooted, 3 + c)
                then(dve.reciprocal(rstd[:, js], root_out[:, js]))
                dve.tensor_tensor(shift[:, js], nmean[:, js], rstd[:, js], ALU.mult).then_inc(s_scale, 1)
                if any(dve_norm(q)[0] for q in gin_steps(c)):
                    dve.wait_ge(s_scale, c + 1)
                for q in gin_steps(c):
                    if dve_norm(q)[0]:
                        for j in range(q * JQ, (q + 1) * JQ):
                            last = dve.tensor_scalar(tab[:, j, :], tab[:, j, :], rstd[:, j:j + 1], shift[:, j:j + 1], ALU.mult, ALU.add)
                        then(last)
                        t = tab[:, q * JQ:(q + 1) * JQ, :]
                        dve.tensor_scalar(t, t, 0.0, None, ALU.max).then_inc(s_norm_v, 1)

            for c in range(GC + 1):
                if c < GC:
                    for q in gin_steps(c):
                        linear_read(1, q)
                        if c >= 2 and q == CUTS[c]:
                            finish(c - 2)
                else:
                    finish(c - 2)
                if c >= 1:
                    dve.wait_ge(s_sum, c)
                    then(ln_stats(c - 1))
                    ln_rstd_start(gin_cols(c - 1))
            finish(GC - 1)
            dve.wait_ge(s_linv, 2 * J)
            fast_pass(2)
            if_far(dve, lambda: sweep(2))

            dve.wait_ge(s_ln, 1)
            dve.tensor_tensor(logz[:, :], esum[:, :], nmax[:, :], ALU.subtract).then_inc(s_logz, 1)
            for w in range(NW):
                dve.wait_ge(s_z2, w + 1)
                last = dve.bn_stats(bn[:, w, :], acc[:, w * SW:(w + 1) * SW])
            then(last)
            then(dve.bn_aggr(bnv[:, 0:2], bn[:, :, :].rearrange("f w k -> f (w k)")))
            dve.tensor_scalar(bnv[:, 2:3], bnv[:, 1:2], EPS, None, ALU.add).then_inc(s_root, 1)
            dve.wait_ge(s_rooted, 3 + GC)
            then(dve.reciprocal(bnv[:, 4:5], bnv[:, 3:4]))
            then(dve.tensor_tensor(bnv[:, 6:7], bnv[:, 4:5], colv[:, 2:3], ALU.mult))
            then(dve.tensor_tensor(bnv[:, 5:6], bnv[:, 0:1], bnv[:, 6:7], ALU.mult))
            dve.tensor_tensor(bnv[:, 7:8], colv[:, 3:4], bnv[:, 5:6], ALU.subtract).then_inc(s_bn, 1)
            for q in range(NQ):
                dve.wait_ge(s_yt, q + 1)
                dve.wait_ge(s_x1, q // QC + 1)
                xs = x_sb[:, q * JQ:(q + 1) * JQ, :]
                dve.tensor_tensor(xs, xs, bank[4 + q % 3][0:PN, 0:JQ * F].rearrange("p (j f) -> p j f", j=JQ),
                                  ALU.add).then_inc(s_ya, 1)


_INS = ['x', 'src', 'dst', 'edge_attr_32', 'edge_weight', 'L0_gnn_W1', 'L0_gnn_b1', 'L0_gnn_W2', 'L0_gnn_b2',
        'L1_gnn_We', 'L1_gnn_be', 'L1_gnn_W1', 'L1_gnn_b1', 'L1_gnn_W2', 'L1_gnn_b2', 'L1_gnn_gamma', 'L1_gnn_beta']


def kernel(**inputs):
    import numpy as _np
    import concourse.bacc as _bacc
    from concourse import mybir as _mybir
    from concourse.bass_utils import run_bass_kernel_spmd as _run

    nc = _bacc.Bacc("TRN2", target_bir_lowering=False, num_devices=1)
    arrays, args = {}, []
    for name in _INS:
        a = _np.ascontiguousarray(inputs[name])
        arrays[f"in_{name}_dram"] = a
        args.append(nc.dram_tensor(f"in_{name}_dram", a.shape, _mybir.dt.from_np(a.dtype), kind="ExternalInput").ap())
    out = nc.dram_tensor("out_0_dram", inputs["x"].shape, _mybir.dt.float32, kind="ExternalOutput").ap()
    build_gnn(nc, *args, out)
    r = _run(nc, [arrays], core_ids=[0])
    return r.results[0]["out_0_dram"]
```
